# Optimizing a Trainium2 kernel written in Bass

```python
import numpy as np
import jax
import jax.numpy as jnp

def _softmax(x, axis=-1):
    return jax.nn.softmax(x, axis=axis)

def _gelu(x):
    return jax.nn.gelu(x, approximate=True)

def _silu(x):
    return jax.nn.silu(x)

def _sigmoid(x):
    return jax.nn.sigmoid(x)

def _layernorm(x, axis=-1, eps=1e-05):
    m = jnp.mean(x, axis=axis, keepdims=True)
    v = jnp.var(x, axis=axis, keepdims=True)
    return (x - m) / jnp.sqrt(v + eps)

def _scatter_add(tgt, idx, src, axis=0):
    return tgt.at[idx].add(src)

def _segment_sum(src, seg, n):
    return jax.ops.segment_sum(src, seg, n)
kernel_name = 'mk_prb_d1_jaxref_r8_3140e0'

def setup_inputs(seed: int=0):
    np.random.seed(seed)
    _w = jnp.asarray

    def _L0_attn_setup():
        import jax, jax.numpy as jnp
        import numpy as np
        CHUNK = 32
        H, DK, DV = (4, 32, 32)
        FORGET_MIN = 0.55
        MAX_FLOOR = 0.075

        def l2norm(x, eps=1e-06):
            return x * jax.lax.rsqrt(jnp.sum(x * x, axis=-1, keepdims=True) + eps)

        def causal_dwconv(x, w):
            b, l, C = x.shape
            K = w.shape[-1]
            xt = jnp.transpose(x, (0, 2, 1))
            y = jax.lax.conv_general_dilated(xt, w[:, None, :], (1,), [(K - 1, 0)], feature_group_count=C)
            return jnp.transpose(y, (0, 2, 1))

        def fir_conv(x, filt):
            b, l, h, d = x.shape
            y = causal_dwconv(x.reshape(b, l, h * d), filt.reshape(h * d, -1))
            return y.reshape(b, l, h, d)

        def delta_rule(q, k, v, beta, lam):
            b, h, L, dk = q.shape
            dv = v.shape[-1]
            c = CHUNK
            n = L // c
            q = l2norm(q)
            k = l2norm(k)
            v = v * beta[..., None]
            kb = k * beta[..., None]
            rs = lambda t: t.reshape(b, h, n, c, -1)
            q, k, v, kb = (rs(q), rs(k), rs(v), rs(kb))
            strict_lower = jnp.tril(jnp.ones((c, c), bool), -1)
            T = jnp.where(strict_lower, -jnp.einsum('bhncd,bhnmd->bhncm', kb, k), 0.0)

            def body(i, A):
                row = A[..., i, :]
                upd = jnp.einsum('bhnc,bhncm->bhnm', row, A)
                new_row = jnp.where(jnp.arange(c) < i, row + upd, row)
                return A.at[..., i, :].set(new_row)
            T = jax.lax.fori_loop(1, c, body, T)
            T = T + jnp.eye(c, dtype=T.dtype)
            u = T @ v
            w = T @ kb
            incl_lower = jnp.tril(jnp.ones((c, c), bool))
            lam_b = lam[None, :, None, None]

            def step(S, xs):
                qi, ki, ui, wi = xs
                attn = jnp.where(incl_lower, jnp.einsum('bhcd,bhmd->bhcm', qi, ki), 0.0)
                u_i = ui - wi @ S
                o_i = qi @ S + attn @ u_i
                S_new = S * lam_b + jnp.einsum('bhcd,bhcv->bhdv', ki, u_i)
                return (S_new, o_i)
            xs = tuple((jnp.moveaxis(t, 2, 0) for t in (q, k, u, w)))
            S0 = jnp.zeros((b, h, dk, dv), q.dtype)
            S, o = jax.lax.scan(step, S0, xs)
            o = jnp.moveaxis(o, 0, 2).reshape(b, h, L, dv)
            return (o, S)

        def fusion_gate(hidden, short, long, delta, value, log_temp, floor_param, W1, b1, W2, b2):

            def stats(t):
                m = t.mean(-1)
                var = t.var(-1)
                mx = t.max(-1)
                l2 = jnp.linalg.norm(t, axis=-1)
                return jnp.stack([m, var, mx, l2], -1)
            b, l = hidden.shape[:2]
            flat = [stats(t).reshape(b, l, -1) for t in (short, long, delta, value)]
            gate_in = jnp.concatenate([hidden] + flat, axis=-1)
            hmid = jax.nn.gelu(gate_in @ W1 + b1, approximate=False)
            logits = (hmid @ W2 + b2).reshape(b, l, H, 4)
            temp = jnp.exp(log_temp)[None, None, :, None]
            raw_p = jax.nn.softmax(logits / temp, axis=-1)
            floor = (jax.nn.sigmoid(floor_param) * MAX_FLOOR)[None, None, :, :]
            clipped = jnp.maximum(raw_p, floor)
            return clipped / clipped.sum(-1, keepdims=True)

        def rms_norm(x, w, eps=1e-05):
            return x * jax.lax.rsqrt(jnp.mean(x * x, axis=-1, keepdims=True) + eps) * w
        key = jax.random.key(seed)
        ks = jax.random.split(key, 20)
        B, L, D = (2, 256, 128)
        s = 0.02
        rn = lambda i, shape, sc=s: jax.random.normal(ks[i], shape, jnp.float32) * sc
        fir_s = jnp.zeros((H, DV, 3)).at[..., -1].set(1.0) + rn(9, (H, DV, 3), 0.007)
        fir_l = jnp.zeros((H, DV, 63)).at[..., -1].set(1.0) + rn(10, (H, DV, 63), 0.007)
        gate_in_dim = D + 16 * H
        b2 = jnp.zeros((H * 4,)).at[H * 3::4].set(2.0)
        return {'hidden_states': jax.random.normal(ks[0], (B, L, D), jnp.float32), 'Wq': rn(1, (D, D)), 'Wk': rn(2, (D, D)), 'Wv': rn(3, (D, D)), 'Wb': rn(4, (D, H)), 'forget_param': jnp.full((H,), 9.2102), 'conv_q': rn(5, (D, 4), 0.3), 'conv_k': rn(6, (D, 4), 0.3), 'conv_v': rn(7, (D, 4), 0.3), 'fir_short_w': fir_s, 'fir_long_w': fir_l, 'log_temp': jnp.log(jnp.full((H,), 1.25)), 'floor_param': jnp.full((H, 4), -2.0), 'W1': rn(11, (gate_in_dim, 2 * D)), 'b1': jnp.zeros((2 * D,)), 'W2': rn(12, (2 * D, H * 4)), 'b2': b2, 'norm_w': jnp.ones((DV,)), 'Wo': rn(13, (D, D))}
    _L0_attn_in = _L0_attn_setup()

    def _L0_ffn_setup():
        import jax, jax.numpy as jnp
        import numpy as np
        DIM = 128
        DEPTH = 6
        HEADS = 16
        DIM_HEAD = 64
        WINDOW = 32
        INNER = HEADS * DIM_HEAD
        DIM_INNER = int(DIM * 4 * 2 / 3)
        QK_SCALE = 8.0

        def shift_tokens(t):
            a, s = jnp.split(t, 2, -1)
            s = jnp.pad(s, ((0, 0), (1, 0), (0, 0)))[:, :-1]
            return jnp.concatenate([a, s], -1)

        def l2norm(t):
            return t / jnp.maximum(jnp.linalg.norm(t, axis=-1, keepdims=True), 1e-12)

        def rotate_half(x):
            x1, x2 = jnp.split(x, 2, -1)
            return jnp.concatenate([-x2, x1], -1)

        def rotary_tables(n):
            half = jnp.arange(0, DIM_HEAD, 2, dtype=jnp.float32)
            inv_freq = 1.0 / 10000.0 ** (half / DIM_HEAD)
            t = jnp.arange(n, dtype=jnp.float32)
            freqs = t[:, None] * inv_freq[None, :]
            freqs = jnp.concatenate([freqs, freqs], -1)
            base_scale = (half + 0.4 * DIM_HEAD) / (1.4 * DIM_HEAD)
            power = (t - n // 2) / (WINDOW // 2)
            scale = base_scale[None, :] ** power[:, None]
            scale = jnp.concatenate([scale, scale], -1)
            return (freqs, scale)

        def local_attention(q, k, v):
            b, h, n, d = q.shape
            w = WINDOW
            nw = n // w
            bq = q.reshape(b, h, nw, w, d)
            bk = k.reshape(b, h, nw, w, d)
            bv = v.reshape(b, h, nw, w, d)

            def look(t):
                p = jnp.pad(t, ((0, 0), (0, 0), (1, 0), (0, 0), (0, 0)))
                return jnp.concatenate([p[:, :, :nw], p[:, :, 1:]], axis=3)
            bk2, bv2 = (look(bk), look(bv))
            seq = jnp.arange(n).reshape(nw, w)
            seq_p = jnp.pad(seq, ((1, 0), (0, 0)), constant_values=-1)
            jt = jnp.concatenate([seq_p[:nw], seq_p[1:]], axis=1)
            it = seq[:, :, None]
            jb = jt[:, None, :]
            mask = (it < jb) | (it > jb + w) | (jb == -1)
            sim = jnp.einsum('bhwie,bhwje->bhwij', bq, bk2) * QK_SCALE
            sim = jnp.where(mask, -jnp.finfo(sim.dtype).max, sim)
            attn = jax.nn.softmax(sim, -1)
            out = jnp.einsum('bhwij,bhwje->bhwie', attn, bv2)
            return out.reshape(b, h, n, d)

        def attn_layer(x, Wqkv, qs, ksc, Wo):
            b, n, _ = x.shape
            qkv = x @ Wqkv
            q, k, v = jnp.split(qkv, 3, -1)
            sh = lambda t: t.reshape(b, n, HEADS, DIM_HEAD).transpose(0, 2, 1, 3)
            q, k, v = (sh(q), sh(k), sh(v))
            q = l2norm(q) * qs
            k = l2norm(k) * ksc
            freqs, scale = rotary_tables(n)
            cos, sin = (jnp.cos(freqs), jnp.sin(freqs))
            q = q * cos * scale + rotate_half(q) * sin * scale
            inv = 1.0 / scale
            k = k * cos * inv + rotate_half(k) * sin * inv
            out = local_attention(q, k, v)
            out = out.transpose(0, 2, 1, 3).reshape(b, n, INNER)
            return out @ Wo

        def ffn_layer(x, g, bln, W1, b1, W2, b2):
            mu = x.mean(-1, keepdims=True)
            var = ((x - mu) ** 2).mean(-1, keepdims=True)
            xn = (x - mu) / jnp.sqrt(var + 1e-05) * g + bln
            hg = xn @ W1 + b1
            a, gate = jnp.split(hg, 2, -1)
            return a * jax.nn.gelu(gate, approximate=False) @ W2 + b2
        key = jax.random.key(seed)
        ks = jax.random.split(key, 8)
        B, N = (2, 256)
        init = lambda k, shape: jax.random.normal(k, shape, jnp.float32) * 0.02
        return {'x': jax.random.normal(ks[0], (B, N, DIM), jnp.float32), 'Wqkv': init(ks[1], (DEPTH, DIM, 3 * INNER)), 'q_scale': jnp.ones((DEPTH, DIM_HEAD), jnp.float32), 'k_scale': jnp.ones((DEPTH, DIM_HEAD), jnp.float32), 'Wo': init(ks[2], (DEPTH, INNER, DIM)), 'ln_g': jnp.ones((DEPTH, DIM), jnp.float32), 'ln_b': jnp.zeros((DEPTH, DIM), jnp.float32), 'W1': init(ks[3], (DEPTH, DIM, 2 * DIM_INNER)), 'b1': jnp.zeros((DEPTH, 2 * DIM_INNER), jnp.float32), 'W2': init(ks[4], (DEPTH, DIM_INNER, DIM)), 'b2': jnp.zeros((DEPTH, DIM), jnp.float32)}
    _L0_ffn_in = _L0_ffn_setup()
    _d = {'L0_attn_hidden_states': _L0_attn_in['hidden_states'], 'L0_attn_Wq': _L0_attn_in['Wq'], 'L0_attn_Wk': _L0_attn_in['Wk'], 'L0_attn_Wv': _L0_attn_in['Wv'], 'L0_attn_Wb': _L0_attn_in['Wb'], 'L0_attn_forget_param': _L0_attn_in['forget_param'], 'L0_attn_conv_q': _L0_attn_in['conv_q'], 'L0_attn_conv_k': _L0_attn_in['conv_k'], 'L0_attn_conv_v': _L0_attn_in['conv_v'], 'L0_attn_fir_short_w': _L0_attn_in['fir_short_w'], 'L0_attn_fir_long_w': _L0_attn_in['fir_long_w'], 'L0_attn_log_temp': _L0_attn_in['log_temp'], 'L0_attn_floor_param': _L0_attn_in['floor_param'], 'L0_attn_W1': _L0_attn_in['W1'], 'L0_attn_b1': _L0_attn_in['b1'], 'L0_attn_W2': _L0_attn_in['W2'], 'L0_attn_b2': _L0_attn_in['b2'], 'L0_attn_norm_w': _L0_attn_in['norm_w'], 'L0_attn_Wo': _L0_attn_in['Wo'], 'L0_ffn_Wqkv': _L0_ffn_in['Wqkv'], 'L0_ffn_q_scale': _L0_ffn_in['q_scale'], 'L0_ffn_k_scale': _L0_ffn_in['k_scale'], 'L0_ffn_Wo': _L0_ffn_in['Wo'], 'L0_ffn_ln_g': _L0_ffn_in['ln_g'], 'L0_ffn_ln_b': _L0_ffn_in['ln_b'], 'L0_ffn_W1': _L0_ffn_in['W1'], 'L0_ffn_b1': _L0_ffn_in['b1'], 'L0_ffn_W2': _L0_ffn_in['W2'], 'L0_ffn_b2': _L0_ffn_in['b2']}
    _x0 = _d['L0_attn_hidden_states']
    _d['L0_attn_hidden_states'] = jax.random.normal(jax.random.fold_in(jax.random.key(seed), 1), (16, 256, 128), dtype=_x0.dtype)
    del _x0
    return _d

def reference(L0_attn_hidden_states, L0_attn_Wq, L0_attn_Wk, L0_attn_Wv, L0_attn_Wb, L0_attn_forget_param, L0_attn_conv_q, L0_attn_conv_k, L0_attn_conv_v, L0_attn_fir_short_w, L0_attn_fir_long_w, L0_attn_log_temp, L0_attn_floor_param, L0_attn_W1, L0_attn_b1, L0_attn_W2, L0_attn_b2, L0_attn_norm_w, L0_attn_Wo, L0_ffn_Wqkv, L0_ffn_q_scale, L0_ffn_k_scale, L0_ffn_Wo, L0_ffn_ln_g, L0_ffn_ln_b, L0_ffn_W1, L0_ffn_b1, L0_ffn_W2, L0_ffn_b2):

    def _L0_attn_ref(hidden_states, Wq, Wk, Wv, Wb, forget_param, conv_q, conv_k, conv_v, fir_short_w, fir_long_w, log_temp, floor_param, W1, b1, W2, b2, norm_w, Wo):
        import jax, jax.numpy as jnp
        import numpy as np
        CHUNK = 32
        H, DK, DV = (4, 32, 32)
        FORGET_MIN = 0.55
        MAX_FLOOR = 0.075

        def l2norm(x, eps=1e-06):
            return x * jax.lax.rsqrt(jnp.sum(x * x, axis=-1, keepdims=True) + eps)

        def causal_dwconv(x, w):
            b, l, C = x.shape
            K = w.shape[-1]
            xt = jnp.transpose(x, (0, 2, 1))
            y = jax.lax.conv_general_dilated(xt, w[:, None, :], (1,), [(K - 1, 0)], feature_group_count=C)
            return jnp.transpose(y, (0, 2, 1))

        def fir_conv(x, filt):
            b, l, h, d = x.shape
            y = causal_dwconv(x.reshape(b, l, h * d), filt.reshape(h * d, -1))
            return y.reshape(b, l, h, d)

        def delta_rule(q, k, v, beta, lam):
            b, h, L, dk = q.shape
            dv = v.shape[-1]
            c = CHUNK
            n = L // c
            q = l2norm(q)
            k = l2norm(k)
            v = v * beta[..., None]
            kb = k * beta[..., None]
            rs = lambda t: t.reshape(b, h, n, c, -1)
            q, k, v, kb = (rs(q), rs(k), rs(v), rs(kb))
            strict_lower = jnp.tril(jnp.ones((c, c), bool), -1)
            T = jnp.where(strict_lower, -jnp.einsum('bhncd,bhnmd->bhncm', kb, k), 0.0)

            def body(i, A):
                row = A[..., i, :]
                upd = jnp.einsum('bhnc,bhncm->bhnm', row, A)
                new_row = jnp.where(jnp.arange(c) < i, row + upd, row)
                return A.at[..., i, :].set(new_row)
            T = jax.lax.fori_loop(1, c, body, T)
            T = T + jnp.eye(c, dtype=T.dtype)
            u = T @ v
            w = T @ kb
            incl_lower = jnp.tril(jnp.ones((c, c), bool))
            lam_b = lam[None, :, None, None]

            def step(S, xs):
                qi, ki, ui, wi = xs
                attn = jnp.where(incl_lower, jnp.einsum('bhcd,bhmd->bhcm', qi, ki), 0.0)
                u_i = ui - wi @ S
                o_i = qi @ S + attn @ u_i
                S_new = S * lam_b + jnp.einsum('bhcd,bhcv->bhdv', ki, u_i)
                return (S_new, o_i)
            xs = tuple((jnp.moveaxis(t, 2, 0) for t in (q, k, u, w)))
            S0 = jnp.zeros((b, h, dk, dv), q.dtype)
            S, o = jax.lax.scan(step, S0, xs)
            o = jnp.moveaxis(o, 0, 2).reshape(b, h, L, dv)
            return (o, S)

        def fusion_gate(hidden, short, long, delta, value, log_temp, floor_param, W1, b1, W2, b2):

            def stats(t):
                m = t.mean(-1)
                var = t.var(-1)
                mx = t.max(-1)
                l2 = jnp.linalg.norm(t, axis=-1)
                return jnp.stack([m, var, mx, l2], -1)
            b, l = hidden.shape[:2]
            flat = [stats(t).reshape(b, l, -1) for t in (short, long, delta, value)]
            gate_in = jnp.concatenate([hidden] + flat, axis=-1)
            hmid = jax.nn.gelu(gate_in @ W1 + b1, approximate=False)
            logits = (hmid @ W2 + b2).reshape(b, l, H, 4)
            temp = jnp.exp(log_temp)[None, None, :, None]
            raw_p = jax.nn.softmax(logits / temp, axis=-1)
            floor = (jax.nn.sigmoid(floor_param) * MAX_FLOOR)[None, None, :, :]
            clipped = jnp.maximum(raw_p, floor)
            return clipped / clipped.sum(-1, keepdims=True)

        def rms_norm(x, w, eps=1e-05):
            return x * jax.lax.rsqrt(jnp.mean(x * x, axis=-1, keepdims=True) + eps) * w
        B, L, D = hidden_states.shape
        q = jax.nn.silu(causal_dwconv(hidden_states @ Wq, conv_q))
        k = jax.nn.silu(causal_dwconv(hidden_states @ Wk, conv_k))
        v = jax.nn.silu(causal_dwconv(hidden_states @ Wv, conv_v))
        beta = jax.nn.sigmoid(hidden_states @ Wb)
        lam = FORGET_MIN + (1.0 - FORGET_MIN) * jax.nn.sigmoid(forget_param)
        to_h = lambda t, d: jnp.transpose(t.reshape(B, L, H, d), (0, 2, 1, 3))
        qh, kh, vh = (to_h(q, DK), to_h(k, DK), to_h(v, DV))
        o_delta, _ = delta_rule(qh, kh, vh, jnp.transpose(beta, (0, 2, 1)), lam)
        delta = jnp.transpose(o_delta, (0, 2, 1, 3))
        v_direct = v.reshape(B, L, H, DV)
        short = fir_conv(v_direct, fir_short_w)
        long = fir_conv(v_direct, fir_long_w)
        p = fusion_gate(hidden_states, short, long, delta, v_direct, log_temp, floor_param, W1, b1, W2, b2)
        o = p[..., 0:1] * short + p[..., 1:2] * long + p[..., 2:3] * delta + p[..., 3:4] * v_direct
        o = rms_norm(o, norm_w)
        return o.reshape(B, L, H * DV) @ Wo

    def _L0_ffn_ref(x, Wqkv, q_scale, k_scale, Wo, ln_g, ln_b, W1, b1, W2, b2):
        import jax, jax.numpy as jnp
        import numpy as np
        DIM = 128
        DEPTH = 6
        HEADS = 16
        DIM_HEAD = 64
        WINDOW = 32
        INNER = HEADS * DIM_HEAD
        DIM_INNER = int(DIM * 4 * 2 / 3)
        QK_SCALE = 8.0

        def shift_tokens(t):
            a, s = jnp.split(t, 2, -1)
            s = jnp.pad(s, ((0, 0), (1, 0), (0, 0)))[:, :-1]
            return jnp.concatenate([a, s], -1)

        def l2norm(t):
            return t / jnp.maximum(jnp.linalg.norm(t, axis=-1, keepdims=True), 1e-12)

        def rotate_half(x):
            x1, x2 = jnp.split(x, 2, -1)
            return jnp.concatenate([-x2, x1], -1)

        def rotary_tables(n):
            half = jnp.arange(0, DIM_HEAD, 2, dtype=jnp.float32)
            inv_freq = 1.0 / 10000.0 ** (half / DIM_HEAD)
            t = jnp.arange(n, dtype=jnp.float32)
            freqs = t[:, None] * inv_freq[None, :]
            freqs = jnp.concatenate([freqs, freqs], -1)
            base_scale = (half + 0.4 * DIM_HEAD) / (1.4 * DIM_HEAD)
            power = (t - n // 2) / (WINDOW // 2)
            scale = base_scale[None, :] ** power[:, None]
            scale = jnp.concatenate([scale, scale], -1)
            return (freqs, scale)

        def local_attention(q, k, v):
            b, h, n, d = q.shape
            w = WINDOW
            nw = n // w
            bq = q.reshape(b, h, nw, w, d)
            bk = k.reshape(b, h, nw, w, d)
            bv = v.reshape(b, h, nw, w, d)

            def look(t):
                p = jnp.pad(t, ((0, 0), (0, 0), (1, 0), (0, 0), (0, 0)))
                return jnp.concatenate([p[:, :, :nw], p[:, :, 1:]], axis=3)
            bk2, bv2 = (look(bk), look(bv))
            seq = jnp.arange(n).reshape(nw, w)
            seq_p = jnp.pad(seq, ((1, 0), (0, 0)), constant_values=-1)
            jt = jnp.concatenate([seq_p[:nw], seq_p[1:]], axis=1)
            it = seq[:, :, None]
            jb = jt[:, None, :]
            mask = (it < jb) | (it > jb + w) | (jb == -1)
            sim = jnp.einsum('bhwie,bhwje->bhwij', bq, bk2) * QK_SCALE
            sim = jnp.where(mask, -jnp.finfo(sim.dtype).max, sim)
            attn = jax.nn.softmax(sim, -1)
            out = jnp.einsum('bhwij,bhwje->bhwie', attn, bv2)
            return out.reshape(b, h, n, d)

        def attn_layer(x, Wqkv, qs, ksc, Wo):
            b, n, _ = x.shape
            qkv = x @ Wqkv
            q, k, v = jnp.split(qkv, 3, -1)
            sh = lambda t: t.reshape(b, n, HEADS, DIM_HEAD).transpose(0, 2, 1, 3)
            q, k, v = (sh(q), sh(k), sh(v))
            q = l2norm(q) * qs
            k = l2norm(k) * ksc
            freqs, scale = rotary_tables(n)
            cos, sin = (jnp.cos(freqs), jnp.sin(freqs))
            q = q * cos * scale + rotate_half(q) * sin * scale
            inv = 1.0 / scale
            k = k * cos * inv + rotate_half(k) * sin * inv
            out = local_attention(q, k, v)
            out = out.transpose(0, 2, 1, 3).reshape(b, n, INNER)
            return out @ Wo

        def ffn_layer(x, g, bln, W1, b1, W2, b2):
            mu = x.mean(-1, keepdims=True)
            var = ((x - mu) ** 2).mean(-1, keepdims=True)
            xn = (x - mu) / jnp.sqrt(var + 1e-05) * g + bln
            hg = xn @ W1 + b1
            a, gate = jnp.split(hg, 2, -1)
            return a * jax.nn.gelu(gate, approximate=False) @ W2 + b2
        for i in range(DEPTH):
            x = attn_layer(shift_tokens(x), Wqkv[i], q_scale[i], k_scale[i], Wo[i]) + x
            x = ffn_layer(shift_tokens(x), ln_g[i], ln_b[i], W1[i], b1[i], W2[i], b2[i]) + x
        return x
    x = L0_attn_hidden_states
    xn = _layernorm(x, axis=-1)
    x = x + _L0_attn_ref(xn, L0_attn_Wq, L0_attn_Wk, L0_attn_Wv, L0_attn_Wb, L0_attn_forget_param, L0_attn_conv_q, L0_attn_conv_k, L0_attn_conv_v, L0_attn_fir_short_w, L0_attn_fir_long_w, L0_attn_log_temp, L0_attn_floor_param, L0_attn_W1, L0_attn_b1, L0_attn_W2, L0_attn_b2, L0_attn_norm_w, L0_attn_Wo) + _L0_ffn_ref(xn, L0_ffn_Wqkv, L0_ffn_q_scale, L0_ffn_k_scale, L0_ffn_Wo, L0_ffn_ln_g, L0_ffn_ln_b, L0_ffn_W1, L0_ffn_b1, L0_ffn_W2, L0_ffn_b2)
    return x

_drawn_inputs = setup_inputs


def setup_inputs(seed=0):
    import zlib

    import numpy as np

    out = dict(_drawn_inputs(seed))
    spreads = {'L0_attn_forget_param': (9.210200309753418, 0.6),
     'L0_attn_log_temp': (0.2231435477733612, 0.6),
     'L0_attn_floor_param': (-2.0, 0.6),
     'L0_attn_b1': (0.0, 2.0),
     'L0_attn_norm_w': (1.0, 0.6),
     'L0_ffn_q_scale': (1.0, 0.6),
     'L0_ffn_k_scale': (1.0, 0.6),
     'L0_ffn_ln_g': (1.0, 0.6),
     'L0_ffn_ln_b': (0.0, 0.8),
     'L0_ffn_b1': (0.0, 0.8),
     'L0_ffn_b2': (0.0, 0.1)}
    factors = {'L0_attn_Wq': 33.368,
     'L0_attn_Wk': 28.216,
     'L0_attn_Wb': 143.347,
     'L0_attn_conv_q': 33.865,
     'L0_attn_conv_k': 28.414,
     'L0_attn_fir_short_w': 200.0,
     'L0_attn_W1': 99.216,
     'L0_attn_W2': 68.015,
     'L0_ffn_W1': 3.66,
     'L0_ffn_W2': 3.595,
     'L0_attn_fir_long_w': 32.471,
     'L0_attn_b2': 64.0}
    for name, (base, spread) in spreads.items():
        noise = np.random.default_rng([zlib.crc32(name.encode()), seed]).standard_normal(out[name].shape)
        drawn = base * np.exp(spread * noise) if base else spread * noise
        out[name] = jnp.asarray(drawn.astype(out[name].dtype))
    for name, factor in factors.items():
        out[name] = (out[name] * factor).astype(out[name].dtype)
    return out
```

```python
from contextlib import ExitStack

import numpy as np

import concourse.bass as bass
from concourse import mybir

F32 = mybir.dt.float32
F32R = mybir.dt.float32r
BF16 = mybir.dt.bfloat16
I32 = mybir.dt.int32
ALU = mybir.AluOpType
ACT = mybir.ActivationFunctionType
AX = mybir.AxisListType

P = 128
NSEQ, L = 16, 256
NT = NSEQ * L // P
DEPTH, HEADS, DH, WIN = 6, 16, 64, 32
INNER = HEADS * DH
NPAIR = HEADS // 2
FFN = 341
FCH = 3
CK = 512
KW = P + WIN
NPAR = 2 * FCH + 3
NEG = -1e30
H, D, C = 4, 32, 32
GS = 4
NG = NSEQ // GS
GT = GS * L
NB = GT // C
PAD = 62
LONG, SHORT, CONV = 63, 3, 4
PE_TAPS = 30
MAGIC = float(0x5F3759DF)
NEWTON = 11


def need(eng, sem, value):
    if isinstance(value, int) and value <= 0:
        return
    eng.wait_ge(sem, value)


def newton_step(nc, eng, k, x, y, t, sem, before):
    if k > 0:
        eng.wait_ge(sem, before + k)
    if k == 0:
        ins = nc.vector.tensor_scalar(t.bitcast(I32), x.bitcast(I32), 1, None, ALU.arith_shift_right)
    elif k == 1:
        ins = nc.vector.tensor_scalar(y.bitcast(I32), t.bitcast(I32), -1.0, MAGIC, ALU.mult, ALU.add)
    elif k % 3 == 2:
        ins = nc.vector.tensor_tensor(t, y, y, ALU.mult)
    elif k % 3 == 0:
        ins = nc.vector.scalar_tensor_tensor(t, t, -0.5, x, ALU.mult, ALU.mult)
    else:
        ins = nc.vector.scalar_tensor_tensor(y, t, 1.5, y, ALU.add, ALU.mult)
    ins.then_inc(sem, 1)


def newton_rsqrt(nc, eng, x, y, t, sem, before):
    for k in range(NEWTON):
        newton_step(nc, eng, k, x, y, t, sem, before)


def normalise_input(nc, x_d, stateT, ident):
    with ExitStack() as stack:
        def sb(name, shape, dt=F32):
            return stack.enter_context(nc.sbuf_tensor(name, shape, dt))

        def sem(name):
            return stack.enter_context(nc.semaphore(name))

        xt = sb("n_x", [P, NT, P])
        xc = sb("n_xc", [P, NT, P])
        xq = sb("n_xq", [P, NT, P])
        mean = sb("n_mean", [P, NT])
        var = sb("n_var", [P, NT])
        rstd = sb("n_rstd", [P, NT])
        tmp = sb("n_tmp", [P, NT])
        ps = [stack.enter_context(nc.psum_tensor(f"n_ps{i}", [P, 4, P], F32)) for i in range(2)]
        s_in, s_sum, s_mean, s_cen, s_sq, s_var, s_nw, s_out, s_turn, s_copy, s_eps = (
            sem("n_" + n) for n in ("in", "sum", "mean", "cen", "sq", "var", "nw", "out", "turn", "copy", "eps"))
        block = stack.enter_context(nc.Block())

        @block.sync
        def _(sp):
            sp.dma_start(xt[:, :, :], x_d.rearrange("b (u p) d -> p (b u) d", p=P)).then_inc(s_in, 16)

        @block.vector
        def _(dve):
            dve.wait_ge(s_in, 16)
            nc.vector.tensor_reduce(mean[:, :], xt[:, :, :], AX.X, ALU.add).then_inc(s_sum, 1)
            dve.wait_ge(s_sum, 1)
            nc.vector.tensor_scalar(mean[:, :], mean[:, :], 1.0 / P, None, ALU.mult).then_inc(s_mean, 1)
            dve.wait_ge(s_mean, 1)
            nc.vector.tensor_tensor(xc[:, :, :], xt[:, :, :], mean[:, :].unsqueeze(2).to_broadcast([P, NT, P]),
                                    ALU.subtract).then_inc(s_cen, 1)
            dve.wait_ge(s_sq, 1)
            nc.vector.tensor_reduce(var[:, :], xq[:, :, :], AX.X, ALU.add).then_inc(s_var, 1)
            dve.wait_ge(s_var, 1)
            nc.vector.tensor_scalar(var[:, :], var[:, :], 1.0 / P, 1e-5, ALU.mult, ALU.add).then_inc(s_eps, 1)
            dve.wait_ge(s_eps, 1)
            newton_rsqrt(nc, dve, var[:, :], rstd[:, :], tmp[:, :], s_nw, 0)
            dve.wait_ge(s_nw, NEWTON)
            nc.vector.tensor_tensor(xc[:, :, :], xc[:, :, :], rstd[:, :].unsqueeze(2).to_broadcast([P, NT, P]),
                                    ALU.mult).then_inc(s_out, 1)

        @block.scalar
        def _(act):
            act.wait_ge(s_cen, 1)
            nc.scalar.activation(xq[:, :, :], xc[:, :, :], ACT.Square).then_inc(s_sq, 1)
            for g in range(NT // 4):
                act.wait_ge(s_turn, g + 1)
                nc.scalar.activation(stateT[:, 2 * g:2 * g + 2, :].rearrange("p b t -> p (b t)"),
                                     ps[g % 2][:, :, :].rearrange("p a t -> p (a t)"), ACT.Copy).then_inc(s_copy, 1)

        @block.tensor
        def _(pe):
            pe.wait_ge(s_out, 1)
            for g in range(NT // 4):
                if g >= 2:
                    pe.wait_ge(s_copy, g - 1)
                for a in range(4):
                    mm = nc.tensor.transpose(ps[g % 2][:, a, :], xc[:, 4 * g + a, :], ident[:, :])
                mm.then_inc(s_turn, 1)


def delta_mixer(nc, x_d, stateT, ident, w, base_d):
    with ExitStack() as stack:
        def sb(name, shape, dt=F32):
            return stack.enter_context(nc.sbuf_tensor(name, shape, dt))

        wproj = sb("d_wproj", [P, 3, P])
        wtap = sb("d_wtap", [P, 3, CONV, P])
        wb = sb("d_wb", [P, H])
        wbx = sb("d_wbx", [P, H, D])
        filt = sb("d_filt", [P, SHORT + LONG])
        diag = sb("d_diag", [P, PE_TAPS, P])
        heads = sb("d_heads", [P, 6])
        hv = sb("d_hv", [P, 8])
        w1a = sb("d_w1a", [P, 2 * P])
        w1b = sb("d_w1b", [P, 2 * P])
        b1 = sb("d_b1", [P, 2])
        w2x = sb("d_w2x", [P, 2, P])
        b2x = sb("d_b2x", [P, 1])
        normw = sb("d_normw", [P, D])
        wout = sb("d_wout", [P, P])
        below = sb("d_below", [P, C])
        upto = sb("d_upto", [P, C])
        qc = sb("d_qc", [P, GT])
        kc = sb("d_kc", [P, GT])
        vpad = sb("d_vpad", [P, GS, PAD + L])
        qk_t = sb("d_qk_t", [P, 2, NB, D])
        beta = sb("d_beta", [P, NB])
        beta_t = sb("d_beta_t", [P, NB, D])
        sqr = sb("d_sqr", [P, 4 * NB, D])
        n2 = sb("d_n2", [P, 2 * NB])
        n2r = sb("d_n2r", [P, 2 * NB])
        n2t = sb("d_n2t", [P, 2 * NB])
        vkb = sb("d_vkb", [P, NB, 2 * D])
        na = sb("d_na", [P, NB, C])
        na_u = sb("d_na_u", [P, C, NB])
        inv = sb("d_inv", [P, C, C])
        prod = sb("d_prod", [P, C * C // 4])
        tT = sb("d_tT", [P, NB, C])
        uu = sb("d_uu", [P, NB, D])
        wT = sb("d_wT", [P, NB, C])
        atT = sb("d_atT", [P, NB, C])
        state = sb("d_state", [P, GS, D])
        ui = sb("d_ui", [P, GS, D])
        shortc = sb("d_shortc", [P, GS, L])
        longc = sb("d_longc", [P, GS, L])
        str4 = sb("d_str4", [P, 4, NB, D])
        cen = sb("d_cen", [P, 4 * NB, D])
        taps = cen[:, 0:3 * CONV * P // D, :].rearrange("p b d -> p (b d)").rearrange("p (a k c) -> p a k c", a=3, k=CONV)
        ssum = sb("d_ssum", [P, 4, NB])
        svar = sb("d_svar", [P, 4, NB])
        smsq = sb("d_smsq", [P, 4, NB])
        stat = sb("d_stat", [P, NB, D])
        statc = sb("d_statc", [P, GT])
        hm = sb("d_hm", [P, 2, GT])
        lg = statc
        lt = sb("d_lt", [P, NB, D])
        pg = sb("d_pg", [P, NB, 4])
        pm = sb("d_pm", [P, NB])
        orms = sb("d_orms", [P, NB])
        orr = sb("d_orr", [P, NB])
        ort = sb("d_ort", [P, NB])
        om = sb("d_om", [P, NB, D])
        oc = sb("d_oc", [P, GT])
        xt = sb("d_xt", [P, GT // P, P])
        res = sb("d_res", [P, GT // P, P])
        ps = stack.enter_context(nc.psum_tensor("d_ps", [P, 8, CK], F32))

        S = {n: stack.enter_context(nc.semaphore("d_" + n)) for n in (
            "loaded", "const", "prep", "x_in", "proj", "silu", "turned_qkv", "beta_ps_turned", "beta", "sq_qk", "n2",
            "n2_steps", "unit_t", "unit_c", "vkb", "kk", "na", "na_u", "inv_init", "inv_steps", "tT",
            "pe_blocks", "blocks_out", "s_zero", "ws", "ui", "od", "scan_s", "o_out", "fir_pe", "fir_steps", "short_steps",
            "fir_sum", "streams", "ssum", "stat_steps", "cen", "cen_sq", "l2", "stat", "statc", "hmid", "gelu",
            "logit", "lg", "lt", "sm_steps", "exped", "mixed", "om", "o_sq", "rms_steps", "o_norm", "oc", "out", "res",
            "stored", "vpad_zero", "hv_act", "hv", "cen_read", "temp")}
        block = stack.enter_context(nc.Block())
        NLOAD = 14

        @block.sync
        def _(sp):
            loads = ((wproj[:, :, :], w["wproj"]), (cen[:, 0:3 * CONV * P // D, :].rearrange("p b d -> p (b d)"),
                                                    w["taps"].to_broadcast([P, 3 * CONV * P])),
                     (wb[:, :], w["wb"]), (filt[:, :], w["filt"]), (heads[:, :], w["heads"]),
                     (w1a[:, :], w["w1"][0:P, :]), (w1b[:, :], w["w1"][P:2 * P, :]), (b1[:, :], w["b1"]),
                     (w2x[:, :, :], w["w2x"]), (b2x[:, :], w["b2x"]),
                     (normw[:, :], w["normw"].to_broadcast([P, D])), (wout[:, :], w["wout"]),
                     (below[:, :], w["below"]), (upto[:, :], w["upto"]))
            for dst, src in loads:
                sp.dma_start(dst, src).then_inc(S["loaded"], 16)
            assert len(loads) == NLOAD
            for g in range(NG):
                need(sp, S["stored"], g * 16)
                sp.dma_start(xt[:, :, :], x_d[g * GS:(g + 1) * GS, :, :].rearrange("b (u p) d -> p (b u) d", p=P))\
                    .then_inc(S["x_in"], 16)
                sp.wait_ge(S["res"], g + 2)
                sp.dma_start(base_d[:, g * (GT // P):(g + 1) * (GT // P), :], res[:, :, :]).then_inc(S["stored"], 16)
            sp.wait_ge(S["stored"], 16 * NG)

        @block.gpsimd
        def _(pool):
            pool.wait_ge(S["loaded"], 16 * NLOAD)
            nc.gpsimd.memset(vpad[:, :, :], 0.0).then_inc(S["vpad_zero"], 1)
            nc.gpsimd.memset(stat[:, :, :], 0.0).then_inc(S["vpad_zero"], 1)
            nc.gpsimd.tensor_tensor(wtap[:, :, :, :], taps, wproj[:, :, :].unsqueeze(2).to_broadcast([P, 3, CONV, P]),
                                    ALU.mult).then_inc(S["prep"], 1)
            nc.gpsimd.tensor_copy(wbx[:, :, :], wb[:, :].unsqueeze(2).to_broadcast([P, H, D])).then_inc(S["prep"], 1)
            nc.gpsimd.tensor_tensor(diag[:, :, :], ident[:, :].unsqueeze(1).to_broadcast([P, PE_TAPS, P]),
                                    filt[:, SHORT + LONG - PE_TAPS:SHORT + LONG].unsqueeze(2).to_broadcast([P, PE_TAPS, P]),
                                    ALU.mult).then_inc(S["prep"], 1)
            with pool.Fori(0, NG) as g:
                pool.wait_ge(S["beta"], g + 1)
                pool.wait_ge(S["unit_t"], g * 2 + 2)
                b3 = beta[:, :].unsqueeze(2).to_broadcast([P, NB, D])
                nc.gpsimd.tensor_tensor(vkb[:, :, 0:D], str4[:, 3, :, :], b3, ALU.mult).then_inc(S["vkb"], 1)
                nc.gpsimd.tensor_tensor(vkb[:, :, D:2 * D], qk_t[:, 1, :, :], b3, ALU.mult).then_inc(S["vkb"], 1)

        @block.scalar
        def _(act):
            act.wait_ge(S["loaded"], 16 * NLOAD)
            act.wait_ge(S["vpad_zero"], 2)
            nc.scalar.activation(hv[:, 0:1], heads[:, 0:1], ACT.Sigmoid).then_inc(S["hv_act"], 1)
            nc.scalar.activation(hv[:, 4:8], heads[:, 2:6], ACT.Sigmoid).then_inc(S["hv_act"], 1)
            nc.scalar.activation(hv[:, 1:2], heads[:, 1:2], ACT.Exp, scale=-1.0).then_inc(S["hv_act"], 1)
            with act.Fori(0, NG) as g:
                for i, dst in enumerate((qc, kc, vpad)):
                    for c in range(2):
                        act.wait_ge(S["proj"], g * 8 + 2 * i + c + 1)
                        if i == 0 and c == 0:
                            act.wait_ge(S["res"], g + 1)
                        if i < 2:
                            nc.scalar.activation(dst[:, c * CK:(c + 1) * CK], ps[:, 2 * i + c, :], ACT.Silu).then_inc(S["silu"], 1)
                        else:
                            nc.scalar.activation(vpad[:, 2 * c:2 * c + 2, PAD:PAD + L],
                                                 ps[:, 2 * i + c, :].rearrange("p (b t) -> p b t", b=2), ACT.Silu)\
                                .then_inc(S["silu"], 1)
                act.wait_ge(S["beta_ps_turned"], g + 1)
                nc.scalar.activation(beta[:, :].unsqueeze(2), beta_t[:, :, 0:1], ACT.Sigmoid).then_inc(S["beta"], 1)
                act.wait_ge(S["turned_qkv"], g * 3 + 3)
                nc.scalar.activation(sqr[:, 0:2 * NB, :], qk_t[:, :, :, :].rearrange("p a b d -> p (a b) d"), ACT.Square)\
                    .then_inc(S["sq_qk"], 1)
                for i, dst in enumerate((uu, wT)):
                    act.wait_ge(S["pe_blocks"], g * 3 + 2 + i)
                    nc.scalar.activation(dst[:, :, :].rearrange("p b d -> p (b d)"),
                                         ps[:, 4 + 2 * i:6 + 2 * i, :].rearrange("p a b -> p (a b)"), ACT.Copy)\
                        .then_inc(S["blocks_out"], 1)
                for n in range(L // C):
                    act.wait_ge(S["od"], g * 8 + n + 1)
                    nc.scalar.activation(str4[:, 2, n:NB:L // C, :], ps[:, 1, 0:GS * D].rearrange("p (b d) -> p b d", b=GS),
                                         ACT.Copy).then_inc(S["o_out"], 1)
                act.wait_ge(S["cen"], g + 1)
                nc.scalar.activation(sqr[:, :, :], cen[:, :, :], ACT.Square).then_inc(S["cen_sq"], 1)
                act.wait_ge(S["stat_steps"], g * 6 + 6)
                nc.scalar.activation(stat[:, :, 3:16:4].rearrange("p b f -> p f b"), smsq[:, :, :], ACT.Sqrt)\
                    .then_inc(S["l2"], 1)
                for t in range(2):
                    for c in range(2):
                        act.wait_ge(S["hmid"], g * 4 + 2 * t + c + 1)
                        nc.scalar.activation(hm[:, c, t * CK:(t + 1) * CK], ps[:, 2 * t + c, :], ACT.Gelu, bias=b1[:, c:c + 1])\
                            .then_inc(S["gelu"], 1)
                for t in range(2):
                    act.wait_ge(S["logit"], g * 2 + t + 1)
                    nc.scalar.activation(lg[:, t * CK:(t + 1) * CK], ps[:, 4 + t, :], ACT.Identity, bias=b2x[:, 0:1])\
                        .then_inc(S["lg"], 1)
                act.wait_ge(S["sm_steps"], g * 10 + 3)
                nc.scalar.activation(pg[:, :, :], pg[:, :, :], ACT.Exp).then_inc(S["exped"], 1)
                act.wait_ge(S["om"], g + 1)
                nc.scalar.activation(sqr[:, 0:NB, :], om[:, :, :], ACT.Square).then_inc(S["o_sq"], 1)

        @block.vector
        def _(dve):
            V = nc.vector
            V.memset(res[:, :, :], 0.0).then_inc(S["res"], 1)
            dve.wait_ge(S["hv_act"], 3)
            V.tensor_scalar(hv[:, 0:1], hv[:, 0:1], 0.45, 0.55, ALU.mult, ALU.add).then_inc(S["hv"], 1)
            V.tensor_scalar(hv[:, 4:8], hv[:, 4:8], 0.075, None, ALU.mult).then_inc(S["hv"], 1)
            dve.wait_ge(S["hv"], 2)
            with dve.Fori(0, NG) as g:
                for i, (src, dst) in enumerate(((qc, qk_t[:, 0, :, :]), (kc, qk_t[:, 1, :, :]))):
                    dve.wait_ge(S["silu"], g * 6 + 2 * i + 2)
                    V.transpose(dst.rearrange("p b d -> p (b d)"), src[:, :]).then_inc(S["turned_qkv"], 1)
                dve.wait_ge(S["silu"], g * 6 + 6)
                V.transpose(str4[:, 3, :, :].rearrange("p (s n) d -> p s (n d)", s=GS), vpad[:, :, PAD:PAD + L])\
                    .then_inc(S["turned_qkv"], 1)
                dve.wait_ge(S["proj"], g * 8 + 8)
                V.transpose(beta_t[:, :, :].rearrange("p b d -> p (b d)"), ps[:, 6:8, :].rearrange("p a b -> p (a b)"))\
                    .then_inc(S["beta_ps_turned"], 1)
                dve.wait_ge(S["sq_qk"], g + 1)
                V.tensor_reduce(n2[:, :], sqr[:, 0:2 * NB, :], AX.X, ALU.add).then_inc(S["n2"], 1)
                dve.wait_ge(S["n2"], g * 2 + 1)
                V.tensor_scalar(n2[:, :], n2[:, :], 1e-6, None, ALU.add).then_inc(S["n2"], 1)
                dve.wait_ge(S["n2"], g * 2 + 2)
                newton_rsqrt(nc, dve, n2[:, :], n2r[:, :], n2t[:, :], S["n2_steps"], g * NEWTON)
                dve.wait_ge(S["n2_steps"], g * NEWTON + NEWTON)
                for i, dst in ((1, kc), (0, qc)):
                    V.tensor_tensor(qk_t[:, i, :, :], qk_t[:, i, :, :],
                                    n2r[:, i * NB:(i + 1) * NB].unsqueeze(2).to_broadcast([P, NB, D]), ALU.mult)\
                        .then_inc(S["unit_t"], 1)
                    dve.wait_ge(S["unit_t"], g * 2 + 2 - i)
                    V.transpose(dst[:, :], qk_t[:, i, :, :].rearrange("p b d -> p (b d)")).then_inc(S["unit_c"], 1)
                dve.wait_ge(S["kk"], g + 1)
                V.tensor_tensor(na[:, :, :], ps[:, 0:2, :].rearrange("p a (b m) -> p (a b) m", m=C),
                                below[:, :].unsqueeze(1).to_broadcast([P, NB, C]), ALU.mult).then_inc(S["na"], 1)
                dve.wait_ge(S["na"], g * 2 + 1)
                dve.wait_ge(S["beta"], g + 1)
                V.tensor_tensor(na[:, :, :], na[:, :, :], beta[:, :].unsqueeze(2).to_broadcast([P, NB, C]), ALU.mult)\
                    .then_inc(S["na"], 1)
                dve.wait_ge(S["na"], g * 2 + 2)
                V.transpose(na_u[:, :, :], na[:, :, :].rearrange("p b m -> p m b")).then_inc(S["na_u"], 1)
                V.memset(inv[:, :, :], 0.0).then_inc(S["inv_init"], 1)
                dve.wait_ge(S["inv_init"], g * 2 + 1)
                V.memset(inv[:, :, :].rearrange("p a b -> p (a b)")[:, 0:C * C:C + 1], 1.0).then_inc(S["inv_init"], 1)
                dve.wait_ge(S["inv_init"], g * 2 + 2)
                dve.wait_ge(S["na_u"], g + 1)
                for k in range(C - 1):
                    n, m = k + 1, C - 1 - k
                    pr = prod[:, 0:n * m].rearrange("p (a b) -> p a b", a=n)
                    V.tensor_tensor(pr, na_u[:, k, k + 1:C].unsqueeze(1).to_broadcast([P, n, m]),
                                    inv[:, 0:n, k].unsqueeze(2).to_broadcast([P, n, m]), ALU.mult).then_inc(S["inv_steps"], 1)
                    dve.wait_ge(S["inv_steps"], g * (2 * C - 2) + 2 * k + 1)
                    V.tensor_tensor(inv[:, 0:n, k + 1:C], inv[:, 0:n, k + 1:C], pr, ALU.add).then_inc(S["inv_steps"], 1)
                    dve.wait_ge(S["inv_steps"], g * (2 * C - 2) + 2 * k + 2)
                V.transpose(tT[:, :, :].rearrange("p b c -> p c b"), inv[:, :, :].rearrange("p j i -> p i j"))\
                    .then_inc(S["tT"], 1)
                dve.wait_ge(S["pe_blocks"], g * 3 + 1)
                V.tensor_tensor(atT[:, :, :], ps[:, 2:4, :].rearrange("p a (b m) -> p (a b) m", m=C),
                                upto[:, :].unsqueeze(1).to_broadcast([P, NB, C]), ALU.mult).then_inc(S["blocks_out"], 1)
                V.memset(state[:, :, :], 0.0).then_inc(S["s_zero"], 1)
                dve.wait_ge(S["s_zero"], g + 1)
                dve.wait_ge(S["blocks_out"], g * 3 + 3)
                for n in range(L // C):
                    dve.wait_ge(S["ws"], g * 8 + n + 1)
                    V.tensor_tensor(ui[:, :, :], uu[:, n:NB:L // C, :], ps[:, 0, 0:GS * D].rearrange("p (b d) -> p b d", b=GS),
                                    ALU.subtract).then_inc(S["ui"], 1)
                    dve.wait_ge(S["od"], g * 8 + n + 1)
                    V.scalar_tensor_tensor(state[:, :, :], state[:, :, :], hv[:, 0:1],
                                           ps[:, 2, 0:GS * D].rearrange("p (b d) -> p b d", b=GS), ALU.mult, ALU.add)\
                        .then_inc(S["scan_s"], 1)
                for k in range(SHORT):
                    x, f = vpad[:, :, PAD - SHORT + 1 + k:PAD - SHORT + 1 + k + L], filt[:, k:k + 1]
                    if k == 0:
                        V.tensor_scalar(shortc[:, :, :], x, f, None, ALU.mult).then_inc(S["short_steps"], 1)
                    else:
                        dve.wait_ge(S["short_steps"], g * SHORT + k)
                        V.scalar_tensor_tensor(shortc[:, :, :], x, f, shortc[:, :, :], ALU.mult, ALU.add)\
                            .then_inc(S["short_steps"], 1)
                for k in range(LONG - PE_TAPS):
                    x, f = vpad[:, :, k:k + L], filt[:, SHORT + k:SHORT + k + 1]
                    if k == 0:
                        V.tensor_scalar(longc[:, :, :], x, f, None, ALU.mult).then_inc(S["fir_steps"], 1)
                    else:
                        dve.wait_ge(S["fir_steps"], g * (LONG - PE_TAPS) + k)
                        V.scalar_tensor_tensor(longc[:, :, :], x, f, longc[:, :, :], ALU.mult, ALU.add)\
                            .then_inc(S["fir_steps"], 1)
                dve.wait_ge(S["fir_steps"], (g + 1) * (LONG - PE_TAPS))
                dve.wait_ge(S["fir_pe"], g + 1)
                V.tensor_tensor(longc[:, :, :], ps[:, 6:8, :].rearrange("p a (b t) -> p (a b) t", b=2), longc[:, :, :], ALU.add)\
                    .then_inc(S["fir_sum"], 1)
                dve.wait_ge(S["short_steps"], (g + 1) * SHORT)
                V.transpose(str4[:, 0, :, :].rearrange("p b d -> p (b d)"), shortc[:, :, :].rearrange("p s t -> p (s t)"))\
                    .then_inc(S["streams"], 1)
                dve.wait_ge(S["fir_sum"], g + 1)
                V.transpose(str4[:, 1, :, :].rearrange("p b d -> p (b d)"), longc[:, :, :].rearrange("p s t -> p (s t)"))\
                    .then_inc(S["streams"], 1)
                dve.wait_ge(S["streams"], g * 2 + 2)
                dve.wait_ge(S["o_out"], g * 8 + 8)
                dve.wait_ge(S["turned_qkv"], g * 3 + 3)
                s4 = str4[:, :, :, :].rearrange("p s b d -> p (s b) d")
                V.tensor_reduce(ssum[:, :, :].rearrange("p s b -> p (s b)"), s4, AX.X, ALU.add).then_inc(S["ssum"], 1)
                V.tensor_reduce(stat[:, :, 2:16:4].rearrange("p b s -> p s b"), str4[:, :, :, :], AX.X, ALU.max)\
                    .then_inc(S["stat"], 1)
                dve.wait_ge(S["ssum"], g + 1)
                V.tensor_scalar(ssum[:, :, :], ssum[:, :, :], 1.0 / D, None, ALU.mult).then_inc(S["stat_steps"], 1)
                dve.wait_ge(S["stat_steps"], g * 6 + 1)
                V.tensor_tensor(cen[:, :, :], s4, ssum[:, :, :].rearrange("p s b -> p (s b)").unsqueeze(2)
                                .to_broadcast([P, 4 * NB, D]), ALU.subtract).then_inc(S["cen"], 1)
                V.tensor_copy(stat[:, :, 0:16:4].rearrange("p b s -> p s b"), ssum[:, :, :]).then_inc(S["stat_steps"], 1)
                V.tensor_tensor(smsq[:, :, :], ssum[:, :, :], ssum[:, :, :], ALU.mult).then_inc(S["stat_steps"], 1)
                dve.wait_ge(S["cen_sq"], g + 1)
                V.tensor_reduce(svar[:, :, :].rearrange("p s b -> p (s b)"), sqr[:, :, :], AX.X, ALU.add).then_inc(S["stat_steps"], 1)
                dve.wait_ge(S["stat_steps"], g * 6 + 4)
                V.tensor_scalar(stat[:, :, 1:16:4].rearrange("p b s -> p s b"), svar[:, :, :], 1.0 / D, None, ALU.mult)\
                    .then_inc(S["stat_steps"], 1)
                V.scalar_tensor_tensor(smsq[:, :, :], smsq[:, :, :], float(D), svar[:, :, :], ALU.mult, ALU.add)\
                    .then_inc(S["stat_steps"], 1)
                dve.wait_ge(S["stat_steps"], g * 6 + 6)
                dve.wait_ge(S["l2"], g + 1)
                dve.wait_ge(S["stat"], g + 1)
                V.transpose(statc[:, :], stat[:, :, :].rearrange("p b f -> p (b f)")).then_inc(S["statc"], 1)
                dve.wait_ge(S["lg"], g * 2 + 2)
                V.transpose(lt[:, :, :].rearrange("p b d -> p (b d)"), lg[:, :]).then_inc(S["lt"], 1)
                dve.wait_ge(S["lt"], g + 1)
                pmb = pm[:, :].unsqueeze(2).to_broadcast([P, NB, 4])
                steps = [0]

                def step(ins):
                    steps[0] += 1
                    ins.then_inc(S["sm_steps"], 1)
                    dve.wait_ge(S["sm_steps"], g * 10 + steps[0])

                step(V.tensor_scalar(pg[:, :, :], lt[:, :, 0:4], hv[:, 1:2], None, ALU.mult))
                step(V.tensor_reduce(pm[:, :], pg[:, :, :], AX.X, ALU.max))
                step(V.tensor_tensor(pg[:, :, :], pg[:, :, :], pmb, ALU.subtract))
                dve.wait_ge(S["exped"], g + 1)
                step(V.tensor_reduce(pm[:, :], pg[:, :, :], AX.X, ALU.add))
                step(V.reciprocal(pm[:, :], pm[:, :]))
                step(V.tensor_tensor(pg[:, :, :], pg[:, :, :], pmb, ALU.mult))
                step(V.tensor_tensor(pg[:, :, :], pg[:, :, :], hv[:, 4:8].unsqueeze(1).to_broadcast([P, NB, 4]), ALU.max))
                step(V.tensor_reduce(pm[:, :], pg[:, :, :], AX.X, ALU.add))
                step(V.reciprocal(pm[:, :], pm[:, :]))
                step(V.tensor_tensor(pg[:, :, :], pg[:, :, :], pmb, ALU.mult))
                for s in range(4):
                    V.tensor_tensor(cen[:, s * NB:(s + 1) * NB, :], str4[:, s, :, :],
                                    pg[:, :, s:s + 1].to_broadcast([P, NB, D]), ALU.mult).then_inc(S["mixed"], 1)
                dve.wait_ge(S["mixed"], g * 4 + 4)
                V.tensor_reduce(om[:, :, :].rearrange("p b d -> p (b d)"), cen[:, :, :].rearrange("p (s b) d -> p (b d) s", s=4),
                                AX.X, ALU.add).then_inc(S["om"], 1)
                dve.wait_ge(S["o_sq"], g + 1)
                V.tensor_reduce(orms[:, :], sqr[:, 0:NB, :], AX.X, ALU.add).then_inc(S["temp"], 1)
                dve.wait_ge(S["temp"], g * 2 + 1)
                V.tensor_scalar(orms[:, :], orms[:, :], 1.0 / D, 1e-5, ALU.mult, ALU.add).then_inc(S["temp"], 1)
                dve.wait_ge(S["temp"], g * 2 + 2)
                newton_rsqrt(nc, dve, orms[:, :], orr[:, :], ort[:, :], S["rms_steps"], g * NEWTON)
                dve.wait_ge(S["rms_steps"], g * NEWTON + NEWTON)
                V.tensor_tensor(om[:, :, :], om[:, :, :], orr[:, :].unsqueeze(2).to_broadcast([P, NB, D]), ALU.mult)\
                    .then_inc(S["o_norm"], 1)
                dve.wait_ge(S["o_norm"], g * 2 + 1)
                V.tensor_tensor(om[:, :, :], om[:, :, :], normw[:, :].unsqueeze(1).to_broadcast([P, NB, D]), ALU.mult)\
                    .then_inc(S["o_norm"], 1)
                dve.wait_ge(S["o_norm"], g * 2 + 2)
                V.transpose(oc[:, :], om[:, :, :].rearrange("p b d -> p (b d)")).then_inc(S["oc"], 1)
                dve.wait_ge(S["out"], g + 1)
                dve.wait_ge(S["x_in"], g * 16 + 16)
                V.tensor_tensor(res[:, :, :], ps[:, 0:2, :].rearrange("p a (b d) -> p (a b) d", b=4), xt[:, :, :], ALU.add)\
                    .then_inc(S["res"], 1)

        @block.tensor
        def _(pe):
            pe.wait_ge(S["prep"], 3)
            pe.wait_ge(S["loaded"], 16 * NLOAD)
            T = nc.tensor
            with pe.Fori(0, NG) as g:
                pe.wait_ge(S["res"], g + 1)
                for i in range(3):
                    for c in range(2):
                        for b in range(2):
                            for k in range(CONV - 1, -1, -1):
                                s = CONV - 1 - k
                                x = stateT[:, bass.ds(g * GS + 2 * c + b, 1), 0:L - s].rearrange("p a t -> p (a t)")
                                mm = T.matmul(ps[:, 2 * i + c, b * L + s:(b + 1) * L], wtap[:, i, k, :], x,
                                              start=s == 0, stop=s == CONV - 1)
                        mm.then_inc(S["proj"], 1)
                for c in range(2):
                    x = stateT[:, bass.ds(g * GS + 2 * c, 2), :].rearrange("p a t -> p (a t)")
                    T.matmul(ps[:, 6 + c, :], wbx[:, :, :].rearrange("p h d -> p (h d)"), x, start=True, stop=True)\
                        .then_inc(S["proj"], 1)

                def blocks(bank, lhs, rhs, sem):
                    T.matmul(ps[:, bank, 0:1], ident[:, :], ident[:, 0:1], start=True, stop=True)
                    for b in range(NB):
                        for h in range(H):
                            r = slice(h * D, (h + 1) * D)
                            mm = T.matmul(ps[r, bank + b // 16, b % 16 * C:(b % 16 + 1) * C], lhs(r, b), rhs(r, b),
                                          start=True, stop=True)
                    mm.then_inc(sem, 1)

                col = lambda t: (lambda r, b: t[r, b * C:(b + 1) * C])
                blk = lambda t: (lambda r, b: t[r, b, :])
                pe.wait_ge(S["unit_c"], g * 2 + 1)
                pe.wait_ge(S["silu"], g * 6 + 2)
                blocks(0, col(kc), col(kc), S["kk"])
                pe.wait_ge(S["unit_c"], g * 2 + 2)
                pe.wait_ge(S["silu"], g * 6 + 4)
                blocks(2, col(kc), col(qc), S["pe_blocks"])
                pe.wait_ge(S["silu"], g * 6 + 6)
                pe.wait_ge(S["beta_ps_turned"], g + 1)
                pe.wait_ge(S["tT"], g + 1)
                pe.wait_ge(S["vkb"], g * 2 + 2)
                blocks(4, blk(tT), lambda r, b: vkb[r, b, 0:D], S["pe_blocks"])
                blocks(6, lambda r, b: vkb[r, b, D:2 * D], blk(tT), S["pe_blocks"])
                pe.wait_ge(S["blocks_out"], g * 3 + 3)
                pe.wait_ge(S["s_zero"], g + 1)
                fir = [(c, k) for c in range(2) for k in range(PE_TAPS)]

                def long_taps(steps):
                    for c, k in steps:
                        o = LONG - PE_TAPS + k
                        mm = T.matmul(ps[:, 6 + c, :].rearrange("p (b t) -> p b t", b=2), diag[:, k, :],
                                      vpad[:, 2 * c:2 * c + 2, o:o + L], start=k == 0, stop=k == PE_TAPS - 1)
                    return mm

                for n in range(L // C):
                    share = fir[n * len(fir) // 8:(n + 1) * len(fir) // 8]
                    if n > 0:
                        pe.wait_ge(S["scan_s"], g * 8 + n)
                    long_taps(share[0:1])
                    for b in range(GS):
                        for h in range(H):
                            r = slice(h * D, (h + 1) * D)
                            mm = T.matmul(ps[r, 0, b * D:(b + 1) * D], wT[r, b * 8 + n, :], state[r, b, :], start=True, stop=True)
                    mm.then_inc(S["ws"], 1)
                    long_taps(share[1:-1])
                    pe.wait_ge(S["ui"], g * 8 + n + 1)
                    if n > 0:
                        pe.wait_ge(S["o_out"], g * 8 + n)
                    last_tap = long_taps(share[-1:])
                    if n == L // C - 1:
                        last_tap.then_inc(S["fir_pe"], 1)
                    for b in range(GS):
                        for h in range(H):
                            r = slice(h * D, (h + 1) * D)
                            T.matmul(ps[r, 1, b * D:(b + 1) * D], qc[r, (b * 8 + n) * C:(b * 8 + n + 1) * C], state[r, b, :],
                                     start=True, stop=False)
                            T.matmul(ps[r, 1, b * D:(b + 1) * D], atT[r, b * 8 + n, :], ui[r, b, :], start=False, stop=True)
                    for b in range(GS):
                        for h in range(H):
                            r = slice(h * D, (h + 1) * D)
                            mm = T.matmul(ps[r, 2, b * D:(b + 1) * D], qk_t[r, 1, b * 8 + n, :], ui[r, b, :],
                                          start=True, stop=True)
                    mm.then_inc(S["od"], 1)
                pe.wait_ge(S["statc"], g + 1)
                pe.wait_ge(S["scan_s"], g * 8 + 8)
                for t in range(2):
                    x = stateT[:, bass.ds(g * GS + 2 * t, 2), :].rearrange("p a t -> p (a t)")
                    for c in range(2):
                        T.matmul(ps[:, 2 * t + c, :], w1a[:, c * P:(c + 1) * P], x, start=True, stop=False)
                        T.matmul(ps[:, 2 * t + c, :], w1b[:, c * P:(c + 1) * P], statc[:, t * CK:(t + 1) * CK],
                                 start=False, stop=True).then_inc(S["hmid"], 1)
                for t in range(2):
                    pe.wait_ge(S["gelu"], g * 4 + 2 * t + 2)
                    for c in range(2):
                        mm = T.matmul(ps[:, 4 + t, :], w2x[:, c, :], hm[:, c, t * CK:(t + 1) * CK], start=c == 0, stop=c == 1)
                    mm.then_inc(S["logit"], 1)
                pe.wait_ge(S["oc"], g + 1)
                for t in range(GT // P):
                    mm = T.matmul(ps[:, t // 4, t % 4 * P:(t % 4 + 1) * P], oc[:, t * P:(t + 1) * P], wout[:, :],
                                  start=True, stop=True)
                mm.then_inc(S["out"], 1)


def local_transformer(nc, stateT, ident, wqkv_d, scales_d, wb_d, par_d, rot_d, mask_d):
    with ExitStack() as stack:
        def sb(name, shape, dt=F32):
            return stack.enter_context(nc.sbuf_tensor(name, shape, dt))

        stage = sb("stage", [P, 3 * INNER + 4 * DH])
        w_hi = sb("w_hi", [P, 3 * INNER], F32R)
        w_lo = sb("w_lo", [P, 3 * INNER], F32R)
        wo = sb("wo", [P, NPAIR, P])
        w1 = sb("w1", [P, 2, FCH, P])
        w2 = sb("w2", [P, FCH, P])
        stage_wo = stage[:, 0:INNER]
        stage_w1 = stage[:, INNER:INNER + 2 * FCH * P]
        stage_w2 = stage[:, INNER + 2 * FCH * P:INNER + 3 * FCH * P]
        par_all = sb("par_all", [P, DEPTH * NPAR])
        par = sb("par", [P, NPAR])
        rot_base = sb("rot_base", [P, 2, 4 * DH])
        rot = sb("rot", [P, 2, 4, DH])
        mask = sb("mask", [P, 2 * P + 2 * KW], BF16)
        ident_b = sb("ident_b", [P, P], BF16)
        mean_w = sb("mean_w", [P, P])
        xs_hi = sb("xs_hi", [P, 2, L], F32R)
        xs_lo = sb("xs_lo", [P, 2, L], F32R)
        rot_a = sb("rot_a", [P, 2, CK])
        rot_b = sb("rot_b", [P, 2, CK])
        sq = sb("sq", [P, CK])
        qk = sb("qk", [P, 8, CK])
        ss = sb("ss", [P, 8 * 8])
        rn = sb("rn", [P, 2, 8 * 8])
        rn_t = sb("rn_t", [P, 8 * 8])
        qT = sb("qT", [P, 2, NPAIR, L])
        kT = sb("kT", [P, 2, NPAIR, 2, L])
        v = sb("v", [P, 2, 2, INNER])
        pr0 = sb("pr0", [P, 4, 2, P])
        pr1 = sb("pr1", [P, 4, 2, L])
        negmax = sb("negmax", [P, 4, 4])
        psums = sb("psums", [P, 4, 4])
        prec = sb("prec", [P, 4, 4])
        pT0 = sb("pT0", [P, 2, 2, KW])
        pT1 = sb("pT1", [P, 2, 2, P])
        oT = sb("oT", [P, 2, NPAIR, L])
        xf = sb("xf", [P, L])
        xc = sb("xc", [P, L])
        xsq = sb("xsq", [P, L])
        xn = sb("xn", [P, L])
        var = sb("var", [P, 2])
        rstd = sb("rstd", [P, 2])
        rstd_t = sb("rstd_t", [P, 2])
        gate = sb("gate", [P, FCH, L])
        hid = sb("hid", [P, FCH, L])

        banks = [stack.enter_context(nc.psum_tensor(f"bank{i}", [P, CK], F32)) for i in range(8)]
        ps_proj, ps_turn, ps_s0, ps_s1, ps_p0, ps_p1, ps_o, ps_c = banks
        ps_s = [ps_s0, ps_s1]
        KEYS = [P, KW]
        MASK = [mask[:, 0:2 * P], mask[:, 2 * P:2 * P + 2 * KW]]

        S = {n: stack.enter_context(nc.semaphore("t_" + n)) for n in (
            "loaded_a", "loaded_b", "loaded_const", "prepared", "conv_hi", "conv_lo", "conv_act", "conv_dve",
            "rot_ready", "xs_hi_ready", "xs_lo_ready", "projected", "rotated", "squared", "summed",
            "ss_floored", "rn_steps", "added", "scaled", "turned", "turned_out", "v_projected", "v_out",
            "scored", "maxed", "exped", "reciped", "normed", "p_turned", "p_turned_out",
            "valued", "values_out", "wo_done", "x_added", "xf_ready", "mean_done", "centred",
            "centred_sq", "var_done", "var_eps", "rstd_steps", "rstd_spread", "x_scaled", "xn_ready",
            "c_mm", "gate_out", "gelu_done", "value_out", "hid_done", "y_done", "layer_out")}

        class Body:

            def __init__(self, layer, base, n, parity, edge=None, first=False, last=False):
                self.layer, self.m, self.n, self.q, self.edge = layer, base + n, n, parity, edge

                def has(k):
                    return not (first and edge + k < 0) and not (last and edge + k > NSEQ - 1)

                self.aq, self.at, self.b, self.bt, self.c2 = (has(k) for k in (2, 1, 0, -1, -2))
                self.switch = edge if edge is not None and not last else None

            def seq(self, k):
                return self.n + k if self.edge is None else (self.edge + k) % NSEQ

        def pipeline(eng, f):
            def layer(l, base, first):
                for e in (-2, -1, 0, 1):
                    f(Body(l, base, e, e % 2, e, first=first))
                with eng.Fori(0, (NSEQ - 4) // 2) as pair:
                    for q in range(2):
                        f(Body(l, base, pair * 2 + (2 + q), q))
            layer(0, 0, True)
            with eng.Fori(1, DEPTH) as l:
                layer(l, l * NSEQ, False)
            for e in (NSEQ - 2, NSEQ - 1, NSEQ, NSEQ + 1):
                f(Body(DEPTH - 1, NSEQ * (DEPTH - 1), e, e % 2, e, last=True))

        def chunk(j):
            return j % 2, j // 2 % 2, j // 4

        def turned_before(j):
            return 3 * (j // 2) + j % 2

        block = stack.enter_context(nc.Block())

        @block.sync
        def _(sp):
            sp.dma_start(par_all[:, :], par_d).then_inc(S["loaded_const"], 16)
            sp.dma_start(rot_base[:, :, :], rot_d.rearrange("(u p) n -> p u n", p=P)).then_inc(S["loaded_const"], 16)
            sp.dma_start(hid[:, :, :].rearrange("p c t -> p (c t)")[:, 0:2 * P + 2 * KW], mask_d).then_inc(S["loaded_const"], 16)
            for l in range(DEPTH):
                need(sp, S["conv_act"], l * 2)
                need(sp, S["conv_dve"], l * 2)
                sp.dma_start(stage[:, 0:3 * INNER], wqkv_d[l, :, :])\
                    .then_inc(S["loaded_a"], 16)
                sp.dma_start(stage[:, 3 * INNER:3 * INNER + 4 * DH],
                             scales_d[l:l + 1, :].to_broadcast([P, 4 * DH])).then_inc(S["loaded_a"], 16)
                sp.wait_ge(S["conv_hi"], l * 6 + 6)
                sp.wait_ge(S["conv_lo"], l * 6 + 6)
                sp.wait_ge(S["rot_ready"], l + 1)
                sp.dma_start(stage[:, 0:INNER + 3 * FCH * P], wb_d[l, :, :])\
                    .then_inc(S["loaded_b"], 16)

        @block.gpsimd
        def _(pool):
            nc.gpsimd.memset(kT[:, :, :, :, :], 0.0).then_inc(S["prepared"], 1)
            nc.gpsimd.memset(pr1[:, :, :, :], 0.0).then_inc(S["prepared"], 1)
            nc.gpsimd.memset(mean_w[:, :], 1.0 / P).then_inc(S["prepared"], 1)
            nc.gpsimd.memset(xf[:, :], 0.0).then_inc(S["prepared"], 1)
            nc.gpsimd.memset(xs_hi[:, :, :].bitcast(F32), 0.0).then_inc(S["prepared"], 1)
            nc.gpsimd.memset(xs_lo[:, :, :].bitcast(F32), 0.0).then_inc(S["prepared"], 1)
            nc.gpsimd.tensor_copy(ident_b[:, :], ident[:, :]).then_inc(S["prepared"], 1)
            pool.wait_ge(S["loaded_const"], 48)
            nc.gpsimd.tensor_copy(mask[:, :], hid[:, :, :].rearrange("p c t -> p (c t)")[:, 0:2 * P + 2 * KW])\
                .then_inc(S["prepared"], 1)

            def body(b):
                m, G, u1, u2 = b.m, b.m * 8, b.m + 1, b.m + 2
                for j in range(8):
                    if b.b if j >= 1 else b.bt:
                        i = (j - 1) % 4
                        need(pool, S["reciped"], G + j)
                        for half, pr in ((0, pr0[:, i, :, :]), (1, pr1[:, i, :, P - WIN:L])):
                            r = prec[:, i, 2 * half:2 * half + 2].unsqueeze(2).to_broadcast([P, 2, KEYS[half]])
                            nc.gpsimd.tensor_tensor(pr, pr, r, ALU.mult).then_inc(S["normed"], 1)
                    if b.at if j < 7 else b.aq:
                        u, c, uq = (u1, j + 1, 1 - b.q) if j < 7 else (u2, 0, b.q)
                        need(pool, S["rn_steps"], u * 2 * NEWTON + (c // 4 + 1) * NEWTON)
                        need(pool, S["added"], u * 8 + (c + 1))
                        x = qk[:, c, :].rearrange("p (h d) -> p h d", h=8)
                        nc.gpsimd.tensor_tensor(x, x, rn[:, uq, 8 * c:8 * c + 8].unsqueeze(2).to_broadcast([P, 8, DH]),
                                                ALU.mult).then_inc(S["scaled"], 1)
                    if b.aq:
                        need(pool, S["rotated"], u2 * 16 + (2 * j + 2))
                        need(pool, S["turned"], u1 * 8 + (j + 1) if b.at else 0)
                        nc.gpsimd.tensor_tensor(qk[:, j, :], rot_a[:, j % 2, :], rot_b[:, j % 2, :], ALU.add)\
                            .then_inc(S["added"], 1)

            pipeline(pool, body)

        @block.scalar
        def _(act):
            act.wait_ge(S["prepared"], 8)

            def convert(b, cols, first_user_done):
                need(act, S["loaded_a"], b.layer * 32 + 32)
                need(act, *first_user_done)
                for c in cols:
                    nc.scalar.activation(w_hi[:, c * CK:(c + 1) * CK], stage[:, c * CK:(c + 1) * CK], ACT.Copy)\
                        .then_inc(S["conv_hi"], 1)

            def body(b):
                m, G, u1, u2, uc = b.m, b.m * 8, b.m + 1, b.m + 2, b.m - 2
                if b.switch == -2:
                    convert(b, (0, 2, 1, 3), (S["projected"], u2 * 8))
                if b.switch == -1:
                    convert(b, (4, 5), (S["v_projected"], u1 * 4))
                if b.switch == 1:
                    need(act, S["loaded_b"], b.layer * 16 + 16)
                    need(act, S["wo_done"], m - 1)
                    nc.scalar.activation(wo[:, :, :].rearrange("p c n -> p (c n)"), stage_wo, ACT.Copy)\
                        .then_inc(S["conv_act"], 1)
                if b.aq:
                    if not (isinstance(b.layer, int) and b.layer == 0):
                        need(act, S["layer_out"], u2 - (NSEQ - 1))
                    need(act, S["v_projected"], (u2 - 1) * 4)
                    src = stateT[:, b.seq(2), :] if b.edge is not None else \
                        stateT[:, bass.ds(b.seq(2), 1), :].rearrange("p a t -> p (a t)")
                    nc.scalar.activation(xs_hi[0:DH, b.q, :], src[0:DH, :], ACT.Copy).then_inc(S["xs_hi_ready"], 1)
                    nc.scalar.activation(xs_hi[DH:P, b.q, 1:L], src[DH:P, 0:L - 1], ACT.Copy)\
                        .then_inc(S["xs_hi_ready"], 1)
                for j in range(8):
                    i = j % 4
                    if b.aq if j >= 1 else b.at:
                        u, c = (u2, j - 1) if j >= 1 else (u1, 7)
                        need(act, S["rotated"], u * 16 + (2 * c + 2))
                        need(act, S["summed"], u * 8 + c)
                        nc.scalar.activation(sq[:, :], ps_proj[:, :], ACT.Square).then_inc(S["squared"], 1)
                    for half in range(2):
                        if b.b:
                            need(act, S["maxed"], G + G + (2 * j + half + 1))
                            if half == 0:
                                need(act, S["p_turned"], G * 2 + (2 * j - 6))
                            for e in range(2):
                                out = pr0[:, i, e, :] if half == 0 else pr1[:, i, e, P - WIN:L]
                                k = 2 * half + e
                                ins = nc.scalar.activation(out, ps_s[half][:, e * KEYS[half]:(e + 1) * KEYS[half]], ACT.Exp,
                                                           bias=negmax[:, i, k:k + 1], accum_out=psums[:, i, k:k + 1])
                            ins.then_inc(S["exped"], 1)
                        if b.c2 and j == 0 and half == 0:
                            need(act, S["x_scaled"], uc + 1)
                            nc.scalar.activation(xn[:, :], xc[:, :], ACT.Identity, bias=par[:, NPAR - 1:NPAR],
                                                 scale=par[:, NPAR - 2:NPAR - 1]).then_inc(S["xn_ready"], 1)
                    if b.bt and j == 5:
                        need(act, S["x_added"], m)
                        need(act, S["centred"], m - 1)
                        src = stateT[:, b.seq(-1), :] if b.edge is not None else \
                            stateT[:, bass.ds(b.seq(-1), 1), :].rearrange("p a t -> p (a t)")
                        nc.scalar.activation(xf[0:DH, :], src[0:DH, :], ACT.Copy).then_inc(S["xf_ready"], 1)
                        nc.scalar.activation(xf[DH:P, 1:L], src[DH:P, 0:L - 1], ACT.Copy).then_inc(S["xf_ready"], 1)
                    if b.bt and j == 6:
                        need(act, S["centred"], m)
                        nc.scalar.activation(xsq[:, :], xc[:, :], ACT.Square).then_inc(S["centred_sq"], 1)
                    if b.b if j >= 2 else b.bt:
                        for n, (dst, src) in enumerate(((pT0[:, j % 2, :, :], ps_p0[:, 0:2 * KW]),
                                                        (pT1[:, j % 2, :, :], ps_p1[:, 0:2 * P]))):
                            need(act, S["p_turned"], G * 2 + (2 * (j - 2) + n + 1))
                            need(act, S["valued"], G + (j - 2 - 1))
                            nc.scalar.activation(dst.rearrange("p e t -> p (e t)"), src, ACT.Copy)\
                                .then_inc(S["p_turned_out"], 1)
                    if b.at:
                        kind, half, grp = chunk(j)
                        need(act, S["turned"], u1 * 8 + (j + 1))
                        need(act, S["scored"], m * 16)
                        src = ps_turn[:, :].rearrange("p (c t) -> p c t", c=4)
                        cols = slice(half * P, (half + 1) * P)
                        if kind == 0:
                            nc.scalar.activation(qT[:, 1 - b.q, 4 * grp:4 * grp + 4, cols], src, ACT.Copy)\
                                .then_inc(S["turned_out"], 1)
                        else:
                            for e in range(2):
                                r = slice(e * DH, (e + 1) * DH)
                                nc.scalar.activation(kT[r, 1 - b.q, 4 * grp:4 * grp + 4, e, cols], src[r, :, :], ACT.Copy)\
                                    .then_inc(S["turned_out"], 1)
                    if b.c2 and j == 2:
                        need(act, S["gate_out"], uc * 3 + 3)
                        nc.scalar.activation(gate[:, :, :], gate[:, :, :], ACT.Gelu).then_inc(S["gelu_done"], 1)
                    if b.switch == 1 and j == 5:
                        need(act, S["y_done"], m - 1)
                        nc.scalar.activation(w1[:, :, :, :].rearrange("p a c n -> p (a c n)"), stage_w1, ACT.Copy)\
                            .then_inc(S["conv_act"], 1)

            pipeline(act, body)

        @block.vector
        def _(dve):
            dve.wait_ge(S["loaded_const"], 48)
            dve.wait_ge(S["prepared"], 8)

            def convert(b, cols, first_conv):
                for n, c in enumerate(cols):
                    need(dve, S["conv_hi"], b.layer * 6 + (first_conv + n + 1))
                    x = slice(c * CK, (c + 1) * CK)
                    nc.vector.tensor_tensor(w_lo[:, x], stage[:, x], w_hi[:, x].bitcast(F32), ALU.subtract)\
                        .then_inc(S["conv_lo"], 1)

            def body(b):
                m, G, u1, u2, uc = b.m, b.m * 8, b.m + 1, b.m + 2, b.m - 2
                if b.switch == -2:
                    need(dve, S["loaded_a"], b.layer * 32 + 32)
                    need(dve, S["rotated"], u2 * 16)
                    nc.vector.tensor_tensor(
                        rot[:, :, :, :].rearrange("p u k d -> p u (k d)"), rot_base[:, :, :],
                        stage[:, 3 * INNER:3 * INNER + 4 * DH].unsqueeze(1).to_broadcast([P, 2, 4 * DH]),
                        ALU.mult).then_inc(S["rot_ready"], 1)
                    convert(b, (0, 2, 1, 3), 0)
                    need(dve, S["rot_ready"], b.layer + 1)
                if b.switch == -1:
                    convert(b, (4, 5), 4)

                def norm_step(j, step):
                    if not (b.at if j < 4 else b.aq) or j % 4 > 1 or (j % 4 == 0 and step < 0):
                        return
                    k = step if j % 4 == 0 else 7 + step
                    u, uq, cols = (u1, 1 - b.q, slice(32, 64)) if j < 4 else (u2, b.q, slice(0, 32))
                    if k == 0:
                        need(dve, S["summed"], u * 8 + (8 if j < 4 else 4))
                        nc.vector.tensor_scalar(ss[:, cols], ss[:, cols], 1e-24, None, ALU.max).then_inc(S["ss_floored"], 1)
                    else:
                        if k == 1:
                            need(dve, S["ss_floored"], u * 2 + (2 if j < 4 else 1))
                        newton_step(nc, dve, k - 1, ss[:, cols], rn[:, uq, cols], rn_t[:, cols], S["rn_steps"],
                                    u * 2 * NEWTON + (NEWTON if j < 4 else 0))

                def deviation_step(k):
                    if k == 0:
                        need(dve, S["var_done"], m)
                        nc.vector.tensor_scalar(var[:, :], ps_c[:, 0:2], 1e-5, None, ALU.add).then_inc(S["var_eps"], 1)
                    elif k <= NEWTON:
                        if k == 1:
                            need(dve, S["var_eps"], m)
                        newton_step(nc, dve, k - 1, var[:, :], rstd[:, :], rstd_t[:, :], S["rstd_steps"], (m - 1) * NEWTON)

                def between(j, place):
                    norm_step(j, place - 2)
                    if b.bt and j == 7:
                        deviation_step(2 * place)
                        deviation_step(2 * place + 1)

                for j in range(8):
                    i = j % 4
                    if b.switch == 1 and j == 6:
                        need(dve, S["conv_dve"], b.layer * 2 + 2)
                    for half in range(2):
                        if b.b:
                            need(dve, S["scored"], G * 2 + (2 * j + half + 1))
                            x = ps_s[half][:, 0:2 * KEYS[half]].rearrange("p (e k) -> p e k", e=2)
                            nc.vector.tensor_reduce(negmax[:, i, 2 * half:2 * half + 2], x, AX.X, ALU.max, negate=True)\
                                .then_inc(S["maxed"], 1)
                        between(j, half)
                    if b.c2:
                        if j == 0:
                            need(dve, S["rstd_spread"], uc + 1)
                            nc.vector.tensor_tensor(xc[:, :], xc[:, :], ps_c[:, 0:L], ALU.mult).then_inc(S["x_scaled"], 1)
                        if j in (1, 2):
                            need(dve, S["c_mm"], uc * 3 + j)
                            for c in ((0, 1) if j == 1 else (2,)):
                                nc.vector.tensor_scalar(gate[:, c, :], ps_c[:, (c % 2) * L:(c % 2 + 1) * L],
                                                        par[:, FCH + c:FCH + c + 1], None, ALU.add).then_inc(S["gate_out"], 1)
                        if j == 2:
                            nc.vector.tensor_scalar(hid[:, 0, :], ps_c[:, L:2 * L], par[:, 0:1], None, ALU.add)\
                                .then_inc(S["value_out"], 1)
                        if j == 4:
                            need(dve, S["y_done"], uc + 1)
                            dst = stateT[:, b.seq(-2), :] if b.edge is not None else \
                                stateT[:, bass.ds(b.seq(-2), 1), :].rearrange("p a t -> p (a t)")
                            nc.vector.scalar_tensor_tensor(dst, ps_c[:, 0:L], par[:, 2 * FCH:2 * FCH + 1], dst,
                                                           ALU.add, ALU.add).then_inc(S["layer_out"], 1)
                    if b.bt:
                        if j == 5:
                            need(dve, S["wo_done"], m)
                            dst = stateT[:, b.seq(-1), :] if b.edge is not None else \
                                stateT[:, bass.ds(b.seq(-1), 1), :].rearrange("p a t -> p (a t)")
                            nc.vector.tensor_tensor(dst, ps_c[:, 0:L], dst, ALU.add).then_inc(S["x_added"], 1)
                        if j == 6:
                            need(dve, S["mean_done"], m)
                            nc.vector.tensor_tensor(xc[:, :], xf[:, :], ps_c[:, 0:L], ALU.subtract).then_inc(S["centred"], 1)
                    if b.at and 3 <= j < 7:
                        half, c = (j - 3) // 2, (j - 3) % 2
                        need(dve, S["v_projected"], u1 * 4 + (j - 3 + 1))
                        need(dve, S["valued"], m * 8)
                        nc.vector.tensor_copy(v[:, 1 - b.q, half, c * CK:(c + 1) * CK], ps_turn[:, :])\
                            .then_inc(S["v_out"], 1)
                    if b.aq and j == 0:
                        need(dve, S["xs_hi_ready"], u2 * 2 + 2)
                        src = stateT[:, b.seq(2), :] if b.edge is not None else \
                            stateT[:, bass.ds(b.seq(2), 1), :].rearrange("p a t -> p (a t)")
                        nc.vector.tensor_tensor(xs_lo[0:DH, b.q, :], src[0:DH, :], xs_hi[0:DH, b.q, :].bitcast(F32),
                                                ALU.subtract).then_inc(S["xs_lo_ready"], 1)
                        nc.vector.tensor_tensor(xs_lo[DH:P, b.q, 1:L], src[DH:P, 0:L - 1],
                                                xs_hi[DH:P, b.q, 1:L].bitcast(F32), ALU.subtract)\
                            .then_inc(S["xs_lo_ready"], 1)
                    if b.aq if j >= 1 else b.at:
                        u, c = (u2, j - 1) if j >= 1 else (u1, 7)
                        need(dve, S["squared"], u * 8 + (c + 1))
                        nc.vector.tensor_reduce(ss[:, 8 * c:8 * c + 8], sq[:, :].rearrange("p (h d) -> p h d", h=8),
                                                AX.X, ALU.add).then_inc(S["summed"], 1)
                    between(j, 2)
                    if b.c2 and j == 3:
                        need(dve, S["gelu_done"], uc + 1)
                        need(dve, S["value_out"], uc + 1)
                        nc.vector.tensor_tensor(hid[:, 0, :], hid[:, 0, :], gate[:, 0, :], ALU.mult).then_inc(S["hid_done"], 1)
                        need(dve, S["c_mm"], uc * 3 + 3)
                        for c in (1, 2):
                            nc.vector.scalar_tensor_tensor(hid[:, c, :], ps_c[:, (c - 1) * L:c * L], par[:, c:c + 1],
                                                           gate[:, c, :], ALU.add, ALU.mult).then_inc(S["hid_done"], 1)
                    if b.b:
                        need(dve, S["exped"], G * 2 + (2 * j + 2))
                        need(dve, S["normed"], G * 2 + (2 * j - 6))
                        nc.vector.reciprocal(prec[:, i, :], psums[:, i, :]).then_inc(S["reciped"], 1)
                    between(j, 3)
                    if b.b if j >= 3 else b.bt:
                        g = j - 3
                        uq = b.q if j >= 3 else 1 - b.q
                        need(dve, S["valued"], G + (g + 1))
                        need(dve, S["wo_done"], m - 1)
                        nc.vector.tensor_copy(oT[:, uq, g % 8, :], ps_o[:, 0:L]).then_inc(S["values_out"], 1)
                    between(j, 4)
                    if b.switch == 1 and j == 5:
                        need(dve, S["loaded_b"], b.layer * 16 + 16)
                        need(dve, S["layer_out"], m - 1)
                        need(dve, S["xn_ready"], m - 1)
                        nc.vector.tensor_copy(w2[:, :, :].rearrange("p c n -> p (c n)"), stage_w2).then_inc(S["conv_dve"], 1)
                        src = par_all[:, 0:NPAR] if isinstance(b.layer, int) else par_all[:, bass.ds(b.layer * NPAR, NPAR)]
                        nc.vector.tensor_copy(par[:, :], src).then_inc(S["conv_dve"], 1)
                    if b.aq:
                        kind, half, grp = chunk(j)
                        need(dve, S["projected"], u2 * 8 + (j + 1))
                        need(dve, S["added"], u2 * 8 + (j - 1))
                        x = ps_proj[:, :].rearrange("p (h a d) -> p h a d", h=8, a=2)
                        cos = rot[:, half, 2 * kind, :].unsqueeze(1).to_broadcast([P, 8, DH])
                        sin = rot[:, half, 2 * kind + 1, :].rearrange("p (a d) -> p a d", a=2).unsqueeze(1)\
                            .to_broadcast([P, 8, 2, DH // 2])
                        nc.vector.tensor_tensor(rot_a[:, j % 2, :].rearrange("p (h d) -> p h d", h=8),
                                                ps_proj[:, :].rearrange("p (h d) -> p h d", h=8), cos, ALU.mult)\
                            .then_inc(S["rotated"], 1)
                    between(j, 5)
                    if b.aq:
                        nc.vector.tensor_tensor(rot_b[:, j % 2, :].rearrange("p (h a d) -> p h a d", h=8, a=2),
                                                x[:, :, ::-1, :], sin, ALU.mult).then_inc(S["rotated"], 1)
                    between(j, 6)

            pipeline(dve, body)

        @block.tensor
        def _(pe):
            pe.wait_ge(S["loaded_const"], 48)
            pe.wait_ge(S["prepared"], 8)

            def project(out, q, half, cols):
                for n, (x, w) in enumerate(((xs_hi, w_hi), (xs_lo, w_hi), (xs_hi, w_lo))):
                    mm = nc.tensor.matmul(out[:, :], x[:, q, half * P:(half + 1) * P], w[:, cols:cols + CK],
                                          start=n == 0, stop=n == 2)
                return mm

            def body(b):
                m, G, u1, u2, uc = b.m, b.m * 8, b.m + 1, b.m + 2, b.m - 2
                for j in range(8):
                    if b.b:
                        if j in (0, 4):
                            need(pe, S["turned_out"], m * 12 + (6 * (j // 4) + 6))
                        for half in range(2):
                            need(pe, S["exped"], G * 2 + (2 * j - 2 + half + 1))
                            kn = KEYS[half]
                            nc.tensor.matmul(ps_s[half][:, 0:2 * kn], ident_b[:, :], MASK[half], start=True, stop=False)
                            for e in range(2):
                                mm = nc.tensor.matmul(ps_s[half][:, e * kn:(e + 1) * kn], qT[:, b.q, j, half * P:(half + 1) * P],
                                                      kT[:, b.q, j, e, (half + 1) * P - kn:(half + 1) * P],
                                                      start=False, stop=e == 1)
                            mm.then_inc(S["scored"], 1)
                    if b.at and 3 <= j < 7:
                        half, c = (j - 3) // 2, (j - 3) % 2
                        need(pe, S["turned_out"], u1 * 12 + turned_before(j))
                        if b.switch == -1 and j in (3, 4):
                            need(pe, S["conv_lo"], b.layer * 6 + (4 + c + 1))
                        project(ps_turn, 1 - b.q, half, 2 * INNER + c * CK).then_inc(S["v_projected"], 1)
                    if b.c2 and j == 0:
                        need(pe, S["rstd_steps"], uc * NEWTON + NEWTON)
                        for c in range(2):
                            mm = nc.tensor.matmul(ps_c[:, c * P:(c + 1) * P], rstd[:, c:c + 1].to_broadcast([P, P]), ident[:, :],
                                                  start=True, stop=True)
                        mm.then_inc(S["rstd_spread"], 1)
                    if b.b if j >= 2 else b.bt:
                        g, i = j - 2, (j - 2) % 4
                        need(pe, S["normed"], G * 2 + (2 * g + 2))
                        need(pe, S["p_turned_out"], G * 2 + (2 * g - 1))
                        for e in range(2):
                            nc.tensor.transpose(ps_p0[:, e * KW:e * KW + P], pr0[:, i, e, :], ident[:, :])
                            mm = nc.tensor.transpose(ps_p0[:, e * KW + P:(e + 1) * KW], pr1[0:WIN, i, e, 0:P],
                                                     ident[0:WIN, 0:WIN])
                        mm.then_inc(S["p_turned"], 1)
                        need(pe, S["p_turned_out"], G * 2 + 2 * g)
                        for e in range(2):
                            mm = nc.tensor.transpose(ps_p1[:, e * P:(e + 1) * P], pr1[:, i, e, P:L], ident[:, :])
                        mm.then_inc(S["p_turned"], 1)
                    if b.b if j >= 3 else b.bt:
                        g = j - 3
                        uq = b.q if j >= 3 else 1 - b.q
                        need(pe, S["p_turned_out"], G * 2 + (2 * g + 2))
                        need(pe, S["v_out"], (m if j >= 3 else m - 1) * 4 + 4)
                        need(pe, S["values_out"], G + g)
                        for e in range(2):
                            r = slice(e * DH, (e + 1) * DH)
                            c = (2 * (g % 8) + e) * DH
                            nc.tensor.matmul(ps_o[r, 0:KW], v[:, uq, 0, c:c + DH], pT0[:, (j - 1) % 2, e, :],
                                             start=True, stop=False, skip_group_check=True)
                            mm = nc.tensor.matmul(ps_o[r, P:L], v[:, uq, 1, c:c + DH], pT1[:, (j - 1) % 2, e, :],
                                                  start=False, stop=True, skip_group_check=True)
                        mm.then_inc(S["valued"], 1)
                    if b.at:
                        need(pe, S["scaled"], u1 * 8 + (j + 1))
                        if 3 <= j < 7:
                            need(pe, S["v_out"], u1 * 4 + (j - 3 + 1))
                        else:
                            need(pe, S["turned_out"], u1 * 12 + turned_before(j))
                        for c in range(4):
                            mm = nc.tensor.transpose(ps_turn[:, c * P:(c + 1) * P], qk[:, j, c * P:(c + 1) * P], ident[:, :])
                        mm.then_inc(S["turned"], 1)
                    if b.aq:
                        kind, half, grp = chunk(j)
                        need(pe, S["rotated"], u2 * 16 + 2 * j)
                        need(pe, S["squared"], u2 * 8 + j)
                        if j == 0:
                            need(pe, S["xs_lo_ready"], u2 * 2 + 2)
                        if b.switch == -2 and j in (0, 1, 4, 5):
                            need(pe, S["conv_lo"], b.layer * 6 + (j + 1 if j < 2 else j - 1))
                        project(ps_proj, b.q, half, kind * INNER + grp * CK).then_inc(S["projected"], 1)
                    if b.switch == 1 and j == 6:
                        need(pe, S["conv_act"], b.layer * 2 + 2)
                        need(pe, S["conv_dve"], b.layer * 2 + 2)
                    if b.c2:
                        if j == 0:
                            need(pe, S["xn_ready"], uc + 1)
                            for c in range(2):
                                mm = nc.tensor.matmul(ps_c[:, c * L:(c + 1) * L], w1[:, 1, c, :], xn[:, :], start=True, stop=True)
                            mm.then_inc(S["c_mm"], 1)
                        if j == 1:
                            need(pe, S["gate_out"], uc * 3 + 2)
                            nc.tensor.matmul(ps_c[:, 0:L], w1[:, 1, 2, :], xn[:, :], start=True, stop=True)
                            nc.tensor.matmul(ps_c[:, L:2 * L], w1[:, 0, 0, :], xn[:, :], start=True, stop=True)\
                                .then_inc(S["c_mm"], 1)
                        if j == 2:
                            need(pe, S["gate_out"], uc * 3 + 3)
                            need(pe, S["value_out"], uc + 1)
                            for c in (1, 2):
                                mm = nc.tensor.matmul(ps_c[:, (c - 1) * L:c * L], w1[:, 0, c, :], xn[:, :], start=True, stop=True)
                            mm.then_inc(S["c_mm"], 1)
                        if j == 3:
                            need(pe, S["hid_done"], uc * 3 + 3)
                            for c in range(FCH):
                                mm = nc.tensor.matmul(ps_c[:, 0:L], w2[:, c, :], hid[:, c, :], start=c == 0, stop=c == FCH - 1)
                            mm.then_inc(S["y_done"], 1)
                    if b.bt:
                        if j == 4:
                            need(pe, S["values_out"], m * 8)
                            need(pe, S["layer_out"], m - 1)
                            if b.switch == 1:
                                need(pe, S["conv_act"], b.layer * 2 + 1)
                            for c in range(NPAIR):
                                mm = nc.tensor.matmul(ps_c[:, 0:L], wo[:, c, :], oT[:, 1 - b.q, c, :],
                                                      start=c == 0, stop=c == NPAIR - 1)
                            mm.then_inc(S["wo_done"], 1)
                        if j == 5:
                            need(pe, S["xf_ready"], m * 2)
                            nc.tensor.matmul(ps_c[:, 0:L], mean_w[:, :], xf[:, :], start=True, stop=True)\
                                .then_inc(S["mean_done"], 1)
                        if j == 6:
                            need(pe, S["centred_sq"], m)
                            for c in range(2):
                                mm = nc.tensor.matmul(ps_c[:, c:c + 1], xsq[:, c * P:(c + 1) * P], mean_w[:, 0:1],
                                                      start=True, stop=True)
                            mm.then_inc(S["var_done"], 1)

            pipeline(pe, body)


def write_output(nc, stateT, ident, base_d, out_d):
    with ExitStack() as stack:
        base = stack.enter_context(nc.sbuf_tensor("o_base", [P, NT, P], F32))
        ps = [stack.enter_context(nc.psum_tensor(f"o_ps{i}", [P, 4, P], F32)) for i in range(2)]
        s_in, s_turn, s_sum, s_out = (stack.enter_context(nc.semaphore("o_" + n)) for n in ("in", "turn", "sum", "out"))
        block = stack.enter_context(nc.Block())
        out_v = out_d.rearrange("b (u p) d -> p (b u) d", p=P)

        @block.sync
        def _(sp):
            sp.dma_start(base[:, :, :], base_d).then_inc(s_in, 16)
            for c in range(4):
                sp.wait_ge(s_sum, 2 * (c + 1))
                sp.dma_start(out_v[:, 8 * c:8 * c + 8, :], base[:, 8 * c:8 * c + 8, :]).then_inc(s_out, 16)
            sp.wait_ge(s_out, 64)

        @block.tensor
        def _(pe):
            for g in range(NT // 4):
                if g >= 2:
                    pe.wait_ge(s_sum, g - 1)
                for a in range(4):
                    t = 4 * g + a
                    mm = nc.tensor.transpose(ps[g % 2][:, a, :], stateT[:, t // 2, t % 2 * P:(t % 2 + 1) * P], ident[:, :])
                mm.then_inc(s_turn, 1)

        @block.vector
        def _(dve):
            dve.wait_ge(s_in, 16)
            for g in range(NT // 4):
                dve.wait_ge(s_turn, g + 1)
                nc.vector.tensor_tensor(base[:, 4 * g:4 * g + 4, :], ps[g % 2][:, :, :], base[:, 4 * g:4 * g + 4, :], ALU.add)\
                    .then_inc(s_sum, 1)


def program(nc, a, out_d):
    stateT = nc.alloc_sbuf_tensor("stateT", [P, NSEQ, L], F32)
    ident = nc.alloc_sbuf_tensor("ident", [P, P], F32)
    base_d = nc.dram_tensor("base_scratch", [P, NT, P], F32, kind="Internal").ap()
    with ExitStack() as stack:
        s_id = stack.enter_context(nc.semaphore("s_id"))
        with nc.Block() as block:
            @block.gpsimd
            def _(pool):
                nc.gpsimd.memset(ident[:, :], 0.0).then_inc(s_id, 1)
                pool.wait_ge(s_id, 1)
                nc.gpsimd.affine_select(out=ident[:, :], in_=ident[:, :], compare_op=ALU.not_equal, fill=1.0,
                                        base=0, pattern=[[-1, P]], channel_multiplier=1).then_inc(s_id, 1)
                pool.wait_ge(s_id, 2)
    normalise_input(nc, a["x"], stateT, ident)
    delta_mixer(nc, a["x"], stateT, ident, a, base_d)
    local_transformer(nc, stateT, ident, a["wqkv"], a["scales"], a["wb_all"], a["par"], a["rot"], a["mask"])
    write_output(nc, stateT, ident, base_d, out_d)


def shape_constants():
    f = np.float32
    half = np.arange(0, DH, 2, dtype=f)
    inv_freq = (f(1.0) / np.power(f(10000.0), half / f(DH))).astype(f)
    t = np.arange(L, dtype=f)
    freqs = t[:, None] * inv_freq[None, :]
    base = (half + f(0.4 * DH)) / f(1.4 * DH)
    power = (t - f(L // 2)) / f(WIN // 2)
    scale = np.power(base[None, :], power[:, None]).astype(f)
    cos, sin = np.cos(freqs).astype(f), np.sin(freqs).astype(f)
    both = lambda m: np.concatenate([m, m], -1)
    turned = lambda m: np.concatenate([-m, m], -1)
    inv = f(1.0) / scale
    rot = np.stack([both(cos * scale) * f(8), turned(sin * scale) * f(8), both(cos * inv), turned(sin * inv)], 1)
    i = np.arange(P)[:, None]
    masks = []
    for keys, first in ((P, 0), (KW, -WIN)):
        gap = i - (np.arange(keys)[None, :] + first)
        masks += [np.where((gap >= 0) & (gap <= WIN), 0.0, NEG)] * 2
    mask = np.concatenate(masks, 1).astype(f)
    r, c = np.arange(P)[:, None] % C, np.arange(C)[None, :]
    return {"rot": np.ascontiguousarray(rot.reshape(L, 4 * DH).astype(f)), "mask": mask,
            "below": np.where(c < r, -1.0, 0.0).astype(f), "upto": np.where(r <= c, 1.0, 0.0).astype(f)}


def lay_out(i):
    g = {k: np.asarray(v) for k, v in i.items()}
    A, B = "L0_attn_", "L0_ffn_"
    z = lambda *s: np.zeros(s, np.float32)
    a = {"x": g[A + "hidden_states"]}
    a["wqkv"] = g[B + "Wqkv"]
    swap = lambda m: np.concatenate([m[:, DH // 2:], m[:, :DH // 2]], 1)
    qs, ks = g[B + "q_scale"], g[B + "k_scale"]
    a["scales"] = np.stack([qs, swap(qs), ks, swap(ks)], 1).reshape(DEPTH, 4 * DH)
    w1 = z(DEPTH, P, 2, FCH * P)
    w1[:, :, :, :FFN] = g[B + "W1"].reshape(DEPTH, P, 2, FFN)
    w2 = z(DEPTH, FCH * P, P)
    w2[:, :FFN] = g[B + "W2"]
    chunks = lambda m, n: m.reshape(DEPTH, n, P, P).transpose(0, 2, 1, 3).reshape(DEPTH, P, n * P)
    a["wb_all"] = np.concatenate([chunks(g[B + "Wo"], NPAIR), w1.reshape(DEPTH, P, 2 * FCH * P), chunks(w2, FCH)], 2)
    b1 = z(DEPTH, 2, FCH * P)
    b1[:, :, :FFN] = g[B + "b1"].reshape(DEPTH, 2, FFN)
    par = np.concatenate([b1.reshape(DEPTH, 2 * FCH, P)] + [g[B + n][:, None] for n in ("b2", "ln_g", "ln_b")], 1)
    a["par"] = par.transpose(2, 0, 1).reshape(P, DEPTH * NPAR)
    a["wproj"] = np.stack([g[A + n] for n in ("Wq", "Wk", "Wv")], 1)
    a["taps"] = np.stack([g[A + n].T for n in ("conv_q", "conv_k", "conv_v")]).reshape(1, 3 * CONV * P)
    a["wb"] = g[A + "Wb"]
    a["filt"] = np.concatenate([g[A + "fir_short_w"].reshape(P, SHORT), g[A + "fir_long_w"].reshape(P, LONG)], 1)
    a["heads"] = np.repeat(np.concatenate([g[A + "forget_param"][:, None], g[A + "log_temp"][:, None],
                                           g[A + "floor_param"]], 1), D, 0)
    ws = z(H, D, 2 * P)
    ws[:, :16] = g[A + "W1"][P:].reshape(4, H, 4, 2 * P).transpose(1, 0, 2, 3).reshape(H, 16, 2 * P)
    a["w1"] = np.concatenate([g[A + "W1"][:P], ws.reshape(P, 2 * P)], 0)
    a["b1"] = g[A + "b1"].reshape(2, P).T
    w2x = z(2 * P, H, D)
    w2x[:, :, :4] = g[A + "W2"].reshape(2 * P, H, 4)
    a["w2x"] = w2x.reshape(2, P, P).transpose(1, 0, 2)
    b2x = z(H, D)
    b2x[:, :4] = g[A + "b2"].reshape(H, 4)
    a["b2x"] = b2x.reshape(P, 1)
    a["normw"] = g[A + "norm_w"].reshape(1, D)
    a["wout"] = g[A + "Wo"]
    a.update(shape_constants())
    return {k: np.ascontiguousarray(v) for k, v in a.items()}


def kernel(**inputs):
    import concourse.bacc as bacc
    from concourse.bass_utils import run_bass_kernel_spmd

    nc = bacc.Bacc("TRN2", target_bir_lowering=False, num_devices=1)
    arrays = lay_out(inputs)
    args = {k: nc.dram_tensor("in_" + k, v.shape, mybir.dt.from_np(v.dtype), kind="ExternalInput").ap()
            for k, v in arrays.items()}
    out = nc.dram_tensor("out", (NSEQ, L, P), F32, kind="ExternalOutput").ap()
    program(nc, args, out)
    r = run_bass_kernel_spmd(nc, [{"in_" + k: v for k, v in arrays.items()}], core_ids=[0])
    return r.results[0]["out"]
```

```python
from contextlib import ExitStack

import numpy as np

import concourse.bass as bass
from concourse import mybir

F32 = mybir.dt.float32
F32R = mybir.dt.float32r
BF16 = mybir.dt.bfloat16
I32 = mybir.dt.int32
ALU = mybir.AluOpType
ACT = mybir.ActivationFunctionType
AX = mybir.AxisListType

P = 128
NSEQ, L = 16, 256
NT = NSEQ * L // P
DEPTH, HEADS, DH, WIN = 6, 16, 64, 32
INNER = HEADS * DH
NPAIR = HEADS // 2
FFN = 341
FCH = 3
CK = 512
KW = P + WIN
NPAR = 2 * FCH + 3
NEG = -1e30
H, D, C = 4, 32, 32
GS = 4
NG = NSEQ // GS
GT = GS * L
NB = GT // C
PAD = 62
LONG, SHORT, CONV = 63, 3, 4
PE_TAPS, POOL_TAPS = 12, 20
DVE_TAPS = LONG - PE_TAPS - POOL_TAPS
MAGIC = float(0x5F3759DF)
NEWTON = 11


def need(eng, sem, value):
    if isinstance(value, int) and value <= 0:
        return
    eng.wait_ge(sem, value)


def newton_step(nc, eng, k, x, y, t, sem, before):
    if k > 0:
        eng.wait_ge(sem, before + k)
    if k == 0:
        ins = nc.vector.tensor_scalar(t.bitcast(I32), x.bitcast(I32), 1, None, ALU.arith_shift_right)
    elif k == 1:
        ins = nc.vector.tensor_scalar(y.bitcast(I32), t.bitcast(I32), -1.0, MAGIC, ALU.mult, ALU.add)
    elif k % 3 == 2:
        ins = nc.vector.tensor_tensor(t, y, y, ALU.mult)
    elif k % 3 == 0:
        ins = nc.vector.scalar_tensor_tensor(t, t, -0.5, x, ALU.mult, ALU.mult)
    else:
        ins = nc.vector.scalar_tensor_tensor(y, t, 1.5, y, ALU.add, ALU.mult)
    ins.then_inc(sem, 1)


def newton_rsqrt(nc, eng, x, y, t, sem, before):
    for k in range(NEWTON):
        newton_step(nc, eng, k, x, y, t, sem, before)


def normalise_input(nc, x_d, stateT, ident):
    with ExitStack() as stack:
        def sb(name, shape, dt=F32):
            return stack.enter_context(nc.sbuf_tensor(name, shape, dt))

        def sem(name):
            return stack.enter_context(nc.semaphore(name))

        xt = sb("n_x", [P, NT, P])
        xc = sb("n_xc", [P, NT, P])
        xq = sb("n_xq", [P, NT, P])
        mean = sb("n_mean", [P, NT])
        var = sb("n_var", [P, NT])
        rstd = sb("n_rstd", [P, NT])
        tmp = sb("n_tmp", [P, NT])
        ps = [stack.enter_context(nc.psum_tensor(f"n_ps{i}", [P, 4, P], F32)) for i in range(2)]
        s_in, s_sum, s_mean, s_cen, s_sq, s_var, s_nw, s_out, s_turn, s_copy, s_eps = (
            sem("n_" + n) for n in ("in", "sum", "mean", "cen", "sq", "var", "nw", "out", "turn", "copy", "eps"))
        block = stack.enter_context(nc.Block())

        @block.sync
        def _(sp):
            sp.dma_start(xt[:, :, :], x_d.rearrange("b (u p) d -> p (b u) d", p=P)).then_inc(s_in, 16)

        @block.vector
        def _(dve):
            dve.wait_ge(s_in, 16)
            nc.vector.tensor_reduce(mean[:, :], xt[:, :, :], AX.X, ALU.add).then_inc(s_sum, 1)
            dve.wait_ge(s_sum, 1)
            nc.vector.tensor_scalar(mean[:, :], mean[:, :], 1.0 / P, None, ALU.mult).then_inc(s_mean, 1)
            dve.wait_ge(s_mean, 1)
            nc.vector.tensor_tensor(xc[:, :, :], xt[:, :, :], mean[:, :].unsqueeze(2).to_broadcast([P, NT, P]),
                                    ALU.subtract).then_inc(s_cen, 1)
            dve.wait_ge(s_sq, 1)
            nc.vector.tensor_reduce(var[:, :], xq[:, :, :], AX.X, ALU.add).then_inc(s_var, 1)
            dve.wait_ge(s_var, 1)
            nc.vector.tensor_scalar(var[:, :], var[:, :], 1.0 / P, 1e-5, ALU.mult, ALU.add).then_inc(s_eps, 1)
            dve.wait_ge(s_eps, 1)
            newton_rsqrt(nc, dve, var[:, :], rstd[:, :], tmp[:, :], s_nw, 0)
            dve.wait_ge(s_nw, NEWTON)
            nc.vector.tensor_tensor(xc[:, :, :], xc[:, :, :], rstd[:, :].unsqueeze(2).to_broadcast([P, NT, P]),
                                    ALU.mult).then_inc(s_out, 1)

        @block.scalar
        def _(act):
            act.wait_ge(s_cen, 1)
            nc.scalar.activation(xq[:, :, :], xc[:, :, :], ACT.Square).then_inc(s_sq, 1)
            for g in range(NT // 4):
                act.wait_ge(s_turn, g + 1)
                nc.scalar.activation(stateT[:, 2 * g:2 * g + 2, :].rearrange("p b t -> p (b t)"),
                                     ps[g % 2][:, :, :].rearrange("p a t -> p (a t)"), ACT.Copy).then_inc(s_copy, 1)

        @block.tensor
        def _(pe):
            pe.wait_ge(s_out, 1)
            for g in range(NT // 4):
                if g >= 2:
                    pe.wait_ge(s_copy, g - 1)
                for a in range(4):
                    mm = nc.tensor.transpose(ps[g % 2][:, a, :], xc[:, 4 * g + a, :], ident[:, :])
                mm.then_inc(s_turn, 1)


def delta_mixer(nc, x_d, stateT, ident, w, base_d):
    with ExitStack() as stack:
        def sb(name, shape, dt=F32):
            return stack.enter_context(nc.sbuf_tensor(name, shape, dt))

        wproj = sb("d_wproj", [P, 3, P])
        wtap = sb("d_wtap", [P, 3, CONV, P])
        wb = sb("d_wb", [P, H])
        wbx = sb("d_wbx", [P, H, D])
        filt = sb("d_filt", [P, SHORT + LONG])
        diag = sb("d_diag", [P, PE_TAPS, P])
        heads = sb("d_heads", [P, 6])
        hv = sb("d_hv", [P, 8])
        w1a = sb("d_w1a", [P, 2 * P])
        w1b = sb("d_w1b", [P, 2 * P])
        b1 = sb("d_b1", [P, 2])
        w2x = sb("d_w2x", [P, 2, P])
        b2x = sb("d_b2x", [P, 1])
        normw = sb("d_normw", [P, D])
        wout = sb("d_wout", [P, P])
        below = sb("d_below", [P, C])
        upto = sb("d_upto", [P, C])
        qc = sb("d_qc", [P, GT])
        kc = sb("d_kc", [P, GT])
        vpad = sb("d_vpad", [P, GS, PAD + L])
        qk_t = sb("d_qk_t", [P, 2, NB, D])
        beta = sb("d_beta", [P, NB])
        beta_t = sb("d_beta_t", [P, NB, D])
        sqr = sb("d_sqr", [P, 4 * NB, D])
        n2 = sb("d_n2", [P, 2 * NB])
        n2r = sb("d_n2r", [P, 2 * NB])
        n2t = sb("d_n2t", [P, 2 * NB])
        vkb = sb("d_vkb", [P, NB, 2 * D])
        na = sb("d_na", [P, NB, C])
        na_u = sb("d_na_u", [P, C, NB])
        inv = sb("d_inv", [P, C, C])
        prod = sb("d_prod", [P, C * C // 4])
        tT = sb("d_tT", [P, NB, C])
        uu = sb("d_uu", [P, NB, D])
        wT = sb("d_wT", [P, NB, C])
        atT = sb("d_atT", [P, NB, C])
        state = sb("d_state", [P, 2, GS, D])
        ui = sb("d_ui", [P, GS, D])
        shortc = sb("d_shortc", [P, GS, L])
        longc = sb("d_longc", [P, GS, L])
        longp = sb("d_longp", [P, GS, L])
        tapped = sb("d_tapped", [P, GS, L])
        str4 = sb("d_str4", [P, 4, NB, D])
        cen = sb("d_cen", [P, 4 * NB, D])
        taps = cen[:, 0:3 * CONV * P // D, :].rearrange("p b d -> p (b d)").rearrange("p (a k c) -> p a k c", a=3, k=CONV)
        ssum = sb("d_ssum", [P, 4, NB])
        svar = sb("d_svar", [P, 4, NB])
        smsq = sb("d_smsq", [P, 4, NB])
        stat = sb("d_stat", [P, NB, D])
        statc = sb("d_statc", [P, GT])
        hm = sb("d_hm", [P, 2, GT])
        lg = statc
        lt = sb("d_lt", [P, NB, D])
        pg = sb("d_pg", [P, NB, 4])
        pm = sb("d_pm", [P, NB])
        orms = sb("d_orms", [P, NB])
        orr = sb("d_orr", [P, NB])
        ort = sb("d_ort", [P, NB])
        om = sb("d_om", [P, NB, D])
        oc = sb("d_oc", [P, GT])
        xt = sb("d_xt", [P, GT // P, P])
        res = sb("d_res", [P, GT // P, P])
        ps = stack.enter_context(nc.psum_tensor("d_ps", [P, 8, CK], F32))

        S = {n: stack.enter_context(nc.semaphore("d_" + n)) for n in (
            "loaded", "const", "prep", "x_in", "proj", "silu", "turned_qkv", "beta_ps_turned", "beta", "sq_qk", "n2",
            "n2_steps", "unit_t", "unit_c", "vkb", "kk", "na", "na_u", "inv_init", "inv_steps", "tT",
            "pe_blocks", "blocks_out", "s_zero", "ws", "ui", "sd", "od", "scan_s", "o_out", "fir_pe", "fir_steps", "short_steps",
            "fir_sum", "streams", "ssum", "mean_steps", "var_steps", "pool_fir", "cen", "cen_sq", "l2", "stat", "statc", "hmid", "gelu",
            "logit", "lg", "lt", "sm_steps", "exped", "mixed", "om", "o_sq", "rms_steps", "o_norm", "oc", "out", "res",
            "stored", "vpad_zero", "hv_act", "hv", "cen_read", "temp")}

        def groups(eng, group):
            with eng.Fori(0, NG - 1) as g:
                group(g, False)
            group(NG - 1, True)

        block = stack.enter_context(nc.Block())
        NLOAD = 14

        @block.sync
        def _(sp):
            loads = ((wproj[:, :, :], w["wproj"]), (cen[:, 0:3 * CONV * P // D, :].rearrange("p b d -> p (b d)"),
                                                    w["taps"].to_broadcast([P, 3 * CONV * P])),
                     (wb[:, :], w["wb"]), (filt[:, :], w["filt"]), (heads[:, :], w["heads"]),
                     (w1a[:, :], w["w1"][0:P, :]), (w1b[:, :], w["w1"][P:2 * P, :]), (b1[:, :], w["b1"]),
                     (w2x[:, :, :], w["w2x"]), (b2x[:, :], w["b2x"]),
                     (normw[:, :], w["normw"].to_broadcast([P, D])), (wout[:, :], w["wout"]),
                     (below[:, :], w["below"]), (upto[:, :], w["upto"]))
            for dst, src in loads:
                sp.dma_start(dst, src).then_inc(S["loaded"], 16)
            assert len(loads) == NLOAD
            for g in range(NG):
                need(sp, S["stored"], g * 16)
                sp.dma_start(xt[:, :, :], x_d[g * GS:(g + 1) * GS, :, :].rearrange("b (u p) d -> p (b u) d", p=P))\
                    .then_inc(S["x_in"], 16)
                sp.wait_ge(S["res"], g + 2)
                sp.dma_start(base_d[:, g * (GT // P):(g + 1) * (GT // P), :], res[:, :, :]).then_inc(S["stored"], 16)
            sp.wait_ge(S["stored"], 16 * NG)

        @block.gpsimd
        def _(pool):
            pool.wait_ge(S["loaded"], 16 * NLOAD)
            nc.gpsimd.memset(vpad[:, :, :], 0.0).then_inc(S["vpad_zero"], 1)
            nc.gpsimd.memset(stat[:, :, :], 0.0).then_inc(S["vpad_zero"], 1)
            nc.gpsimd.tensor_tensor(wtap[:, :, :, :], taps, wproj[:, :, :].unsqueeze(2).to_broadcast([P, 3, CONV, P]),
                                    ALU.mult).then_inc(S["prep"], 1)
            nc.gpsimd.tensor_copy(wbx[:, :, :], wb[:, :].unsqueeze(2).to_broadcast([P, H, D])).then_inc(S["prep"], 1)
            nc.gpsimd.tensor_tensor(diag[:, :, :], ident[:, :].unsqueeze(1).to_broadcast([P, PE_TAPS, P]),
                                    filt[:, SHORT + LONG - PE_TAPS:SHORT + LONG].unsqueeze(2).to_broadcast([P, PE_TAPS, P]),
                                    ALU.mult).then_inc(S["prep"], 1)
            with pool.Fori(0, NG) as g:
                pool.wait_ge(S["beta"], g + 1)
                pool.wait_ge(S["unit_t"], g * 2 + 2)
                pool.wait_ge(S["turned_qkv"], g * 3 + 3)
                b3 = beta[:, :].unsqueeze(2).to_broadcast([P, NB, D])
                nc.gpsimd.tensor_tensor(vkb[:, :, 0:D], str4[:, 3, :, :], b3, ALU.mult).then_inc(S["vkb"], 1)
                nc.gpsimd.tensor_tensor(vkb[:, :, D:2 * D], qk_t[:, 1, :, :], b3, ALU.mult).then_inc(S["vkb"], 1)
                pool.wait_ge(S["silu"], g * 6 + 6)
                done = 0
                for k in range(DVE_TAPS, DVE_TAPS + POOL_TAPS):
                    x = vpad[:, :, k:k + L]
                    f = filt[:, SHORT + k:SHORT + k + 1].unsqueeze(2).to_broadcast([P, GS, L])
                    first = k == DVE_TAPS
                    if not first:
                        pool.wait_ge(S["pool_fir"], g * (2 * POOL_TAPS - 1) + done)
                    nc.gpsimd.tensor_tensor(longp[:, :, :] if first else tapped[:, :, :], x, f, ALU.mult)\
                        .then_inc(S["pool_fir"], 1)
                    done += 1
                    if not first:
                        pool.wait_ge(S["pool_fir"], g * (2 * POOL_TAPS - 1) + done)
                        nc.gpsimd.tensor_tensor(longp[:, :, :], longp[:, :, :], tapped[:, :, :], ALU.add)\
                            .then_inc(S["pool_fir"], 1)
                        done += 1

        @block.scalar
        def _(act):
            act.wait_ge(S["loaded"], 16 * NLOAD)
            act.wait_ge(S["vpad_zero"], 2)
            nc.scalar.activation(hv[:, 0:1], heads[:, 0:1], ACT.Sigmoid).then_inc(S["hv_act"], 1)
            nc.scalar.activation(hv[:, 4:8], heads[:, 2:6], ACT.Sigmoid).then_inc(S["hv_act"], 1)
            nc.scalar.activation(hv[:, 1:2], heads[:, 1:2], ACT.Exp, scale=-1.0).then_inc(S["hv_act"], 1)

            def silu_qk(g):
                for i, dst in enumerate((qc, kc)):
                    for c in range(2):
                        act.wait_ge(S["proj"], g * 8 + 2 * i + c + 1)
                        nc.scalar.activation(dst[:, c * CK:(c + 1) * CK], ps[:, 4 + 2 * i + c, :], ACT.Silu)\
                            .then_inc(S["silu"], 1)

            def square_qk(g):
                for i, own in ((0, slice(0, NB)), (1, slice(3 * NB, 4 * NB))):
                    act.wait_ge(S["turned_qkv"], g * 3 + i + 1)
                    nc.scalar.activation(sqr[:, own, :], qk_t[:, i, :, :], ACT.Square).then_inc(S["sq_qk"], 1)

            def silu_v(g):
                for c in range(2):
                    act.wait_ge(S["proj"], g * 8 + 4 + c + 1)
                    nc.scalar.activation(vpad[:, 2 * c:2 * c + 2, PAD:PAD + L],
                                         ps[:, 4 + c, :].rearrange("p (b t) -> p b t", b=2), ACT.Silu).then_inc(S["silu"], 1)

            def sigmoid_beta(g):
                act.wait_ge(S["beta_ps_turned"], g + 1)
                nc.scalar.activation(beta[:, :].unsqueeze(2), beta_t[:, :, 0:1], ACT.Sigmoid).then_inc(S["beta"], 1)

            def group(g, last):
                for i, (dst, stream) in enumerate(((uu, 3), (wT, 0))):
                    act.wait_ge(S["cen"], g * 3 + i + 1)
                    own = slice(stream * NB, (stream + 1) * NB)
                    nc.scalar.activation(sqr[:, own, :], cen[:, own, :], ACT.Square).then_inc(S["cen_sq"], 1)
                    act.wait_ge(S["pe_blocks"], g * 3 + 2 + i)
                    nc.scalar.activation(dst[:, :, :].rearrange("p b d -> p (b d)"),
                                         ps[:, 4 - 2 * i:6 - 2 * i, :].rearrange("p a b -> p (a b)"), ACT.Copy)\
                        .then_inc(S["blocks_out"], 1)
                for n in range(L // C):
                    act.wait_ge(S["od"], g * 8 + n + 1)
                    nc.scalar.activation(str4[:, 2, n:NB:L // C, :], ps[:, 1, 0:GS * D].rearrange("p (b d) -> p b d", b=GS),
                                         ACT.Copy).then_inc(S["o_out"], 1)
                if not last:
                    silu_qk(g + 1)
                act.wait_ge(S["cen"], g * 3 + 3)
                nc.scalar.activation(sqr[:, NB:3 * NB, :], cen[:, NB:3 * NB, :], ACT.Square).then_inc(S["cen_sq"], 1)
                if not last:
                    square_qk(g + 1)
                act.wait_ge(S["var_steps"], g * 9 + 9)
                nc.scalar.activation(stat[:, :, 3:16:4].rearrange("p b f -> p f b"), smsq[:, :, :], ACT.Sqrt)\
                    .then_inc(S["l2"], 1)
                for t in range(2):
                    for c in range(2):
                        act.wait_ge(S["hmid"], g * 4 + 2 * t + c + 1)
                        nc.scalar.activation(hm[:, c, t * CK:(t + 1) * CK], ps[:, 2 * t + c, :], ACT.Gelu, bias=b1[:, c:c + 1])\
                            .then_inc(S["gelu"], 1)
                for t in range(2):
                    act.wait_ge(S["logit"], g * 2 + t + 1)
                    nc.scalar.activation(lg[:, t * CK:(t + 1) * CK], ps[:, 2 * t, :], ACT.Identity, bias=b2x[:, 0:1])\
                        .then_inc(S["lg"], 1)
                act.wait_ge(S["sm_steps"], g * 10 + 3)
                nc.scalar.activation(pg[:, :, :], pg[:, :, :], ACT.Exp).then_inc(S["exped"], 1)
                if not last:
                    silu_v(g + 1)
                act.wait_ge(S["om"], g + 1)
                nc.scalar.activation(sqr[:, 0:NB, :], om[:, :, :], ACT.Square).then_inc(S["o_sq"], 1)
                if not last:
                    sigmoid_beta(g + 1)

            silu_qk(0)
            square_qk(0)
            silu_v(0)
            sigmoid_beta(0)
            groups(act, group)

        @block.vector
        def _(dve):
            V = nc.vector
            V.memset(res[:, :, :], 0.0).then_inc(S["res"], 1)
            dve.wait_ge(S["hv_act"], 3)
            V.tensor_scalar(hv[:, 0:1], hv[:, 0:1], 0.45, 0.55, ALU.mult, ALU.add).then_inc(S["hv"], 1)
            V.tensor_scalar(hv[:, 4:8], hv[:, 4:8], 0.075, None, ALU.mult).then_inc(S["hv"], 1)
            dve.wait_ge(S["hv"], 2)

            def turn_qk(g):
                for i, src in enumerate((qc, kc)):
                    dve.wait_ge(S["silu"], g * 6 + 2 * i + 2)
                    V.transpose(qk_t[:, i, :, :].rearrange("p b d -> p (b d)"), src[:, :]).then_inc(S["turned_qkv"], 1)

            def unit_qk(g):
                for i, own in ((0, slice(0, NB)), (1, slice(3 * NB, 4 * NB))):
                    dve.wait_ge(S["sq_qk"], g * 2 + i + 1)
                    V.tensor_reduce(n2[:, i * NB:(i + 1) * NB], sqr[:, own, :], AX.X, ALU.add).then_inc(S["n2"], 1)
                dve.wait_ge(S["n2"], g * 3 + 2)
                V.tensor_scalar(n2[:, :], n2[:, :], 1e-6, None, ALU.add).then_inc(S["n2"], 1)
                dve.wait_ge(S["n2"], g * 3 + 3)
                newton_rsqrt(nc, dve, n2[:, :], n2r[:, :], n2t[:, :], S["n2_steps"], g * NEWTON)
                dve.wait_ge(S["n2_steps"], g * NEWTON + NEWTON)
                for i, dst in ((1, kc), (0, qc)):
                    V.tensor_tensor(qk_t[:, i, :, :], qk_t[:, i, :, :],
                                    n2r[:, i * NB:(i + 1) * NB].unsqueeze(2).to_broadcast([P, NB, D]), ALU.mult)\
                        .then_inc(S["unit_t"], 1)
                    dve.wait_ge(S["unit_t"], g * 2 + 2 - i)
                    V.transpose(dst[:, :], qk_t[:, i, :, :].rearrange("p b d -> p (b d)")).then_inc(S["unit_c"], 1)

            def turn_beta(g):
                dve.wait_ge(S["proj"], g * 8 + 8)
                V.transpose(beta_t[:, :, :].rearrange("p b d -> p (b d)"), ps[:, 6:8, :].rearrange("p a b -> p (a b)"))\
                    .then_inc(S["beta_ps_turned"], 1)

            def turn_v(g):
                dve.wait_ge(S["silu"], g * 6 + 6)
                V.transpose(str4[:, 3, :, :].rearrange("p (s n) d -> p s (n d)", s=GS), vpad[:, :, PAD:PAD + L])\
                    .then_inc(S["turned_qkv"], 1)

            def below_diagonal(g):
                dve.wait_ge(S["kk"], g + 1)
                V.tensor_tensor(na[:, :, :], ps[:, 2:4, :].rearrange("p a (b m) -> p (a b) m", m=C),
                                below[:, :].unsqueeze(1).to_broadcast([P, NB, C]), ALU.mult).then_inc(S["na"], 1)
                dve.wait_ge(S["na"], g * 2 + 1)
                dve.wait_ge(S["beta"], g + 1)
                V.tensor_tensor(na[:, :, :], na[:, :, :], beta[:, :].unsqueeze(2).to_broadcast([P, NB, C]), ALU.mult)\
                    .then_inc(S["na"], 1)

            def group(g, last):
                dve.wait_ge(S["na"], g * 2 + 2)
                V.transpose(na_u[:, :, :], na[:, :, :].rearrange("p b m -> p m b")).then_inc(S["na_u"], 1)
                V.memset(inv[:, :, :], 0.0).then_inc(S["inv_init"], 1)
                dve.wait_ge(S["inv_init"], g * 2 + 1)
                V.memset(inv[:, :, :].rearrange("p a b -> p (a b)")[:, 0:C * C:C + 1], 1.0).then_inc(S["inv_init"], 1)
                dve.wait_ge(S["inv_init"], g * 2 + 2)
                dve.wait_ge(S["na_u"], g + 1)
                for k in range(C - 1):
                    n, m = k + 1, C - 1 - k
                    pr = prod[:, 0:n * m].rearrange("p (a b) -> p a b", a=n)
                    V.tensor_tensor(pr, na_u[:, k, k + 1:C].unsqueeze(1).to_broadcast([P, n, m]),
                                    inv[:, 0:n, k].unsqueeze(2).to_broadcast([P, n, m]), ALU.mult).then_inc(S["inv_steps"], 1)
                    dve.wait_ge(S["inv_steps"], g * (2 * C - 2) + 2 * k + 1)
                    V.tensor_tensor(inv[:, 0:n, k + 1:C], inv[:, 0:n, k + 1:C], pr, ALU.add).then_inc(S["inv_steps"], 1)
                    dve.wait_ge(S["inv_steps"], g * (2 * C - 2) + 2 * k + 2)
                V.transpose(tT[:, :, :].rearrange("p b c -> p c b"), inv[:, :, :].rearrange("p j i -> p i j"))\
                    .then_inc(S["tT"], 1)
                dve.wait_ge(S["pe_blocks"], g * 3 + 1)
                V.tensor_tensor(atT[:, :, :], ps[:, 0:2, :].rearrange("p a (b m) -> p (a b) m", m=C),
                                upto[:, :].unsqueeze(1).to_broadcast([P, NB, C]), ALU.mult).then_inc(S["blocks_out"], 1)

                def mean_of(s0, s1, call):
                    st = str4[:, s0:s1, :, :].rearrange("p s b d -> p (s b) d")
                    flat = ssum[:, s0:s1, :].rearrange("p s b -> p (s b)")
                    n = g * 3 + call
                    V.tensor_reduce(flat, st, AX.X, ALU.add).then_inc(S["ssum"], 1)
                    V.tensor_reduce(stat[:, :, 4 * s0 + 2:4 * s1:4].rearrange("p b s -> p s b"), str4[:, s0:s1, :, :],
                                    AX.X, ALU.max).then_inc(S["stat"], 1)
                    dve.wait_ge(S["ssum"], n + 1)
                    V.tensor_scalar(flat, flat, 1.0 / D, None, ALU.mult).then_inc(S["mean_steps"], 1)
                    dve.wait_ge(S["mean_steps"], n * 3 + 1)
                    V.tensor_tensor(cen[:, s0 * NB:s1 * NB, :], st, flat.unsqueeze(2).to_broadcast([P, (s1 - s0) * NB, D]),
                                    ALU.subtract).then_inc(S["cen"], 1)
                    V.tensor_copy(stat[:, :, 4 * s0:4 * s1:4].rearrange("p b s -> p s b"), ssum[:, s0:s1, :])\
                        .then_inc(S["mean_steps"], 1)
                    V.tensor_tensor(smsq[:, s0:s1, :], ssum[:, s0:s1, :], ssum[:, s0:s1, :], ALU.mult)\
                        .then_inc(S["mean_steps"], 1)

                def variance_of(s0, s1, call):
                    n = g * 3 + call
                    dve.wait_ge(S["cen_sq"], n + 1)
                    V.tensor_reduce(svar[:, s0:s1, :].rearrange("p s b -> p (s b)"), sqr[:, s0 * NB:s1 * NB, :],
                                    AX.X, ALU.add).then_inc(S["var_steps"], 1)
                    dve.wait_ge(S["var_steps"], n * 3 + 1)
                    dve.wait_ge(S["mean_steps"], n * 3 + 3)
                    V.tensor_scalar(stat[:, :, 4 * s0 + 1:4 * s1:4].rearrange("p b s -> p s b"), svar[:, s0:s1, :],
                                    1.0 / D, None, ALU.mult).then_inc(S["var_steps"], 1)
                    V.scalar_tensor_tensor(smsq[:, s0:s1, :], smsq[:, s0:s1, :], float(D), svar[:, s0:s1, :],
                                           ALU.mult, ALU.add).then_inc(S["var_steps"], 1)

                dve.wait_ge(S["turned_qkv"], g * 3 + 3)
                mean_of(3, 4, 0)
                for k in range(SHORT):
                    x, f = vpad[:, :, PAD - SHORT + 1 + k:PAD - SHORT + 1 + k + L], filt[:, k:k + 1]
                    if k == 0:
                        V.tensor_scalar(shortc[:, :, :], x, f, None, ALU.mult).then_inc(S["short_steps"], 1)
                    else:
                        dve.wait_ge(S["short_steps"], g * SHORT + k)
                        V.scalar_tensor_tensor(shortc[:, :, :], x, f, shortc[:, :, :], ALU.mult, ALU.add)\
                            .then_inc(S["short_steps"], 1)
                dve.wait_ge(S["short_steps"], (g + 1) * SHORT)
                V.transpose(str4[:, 0, :, :].rearrange("p b d -> p (b d)"), shortc[:, :, :].rearrange("p s t -> p (s t)"))\
                    .then_inc(S["streams"], 1)
                dve.wait_ge(S["streams"], g * 2 + 1)
                mean_of(0, 1, 1)
                variance_of(3, 4, 0)
                variance_of(0, 1, 1)

                def long_taps(taps):
                    for k in taps:
                        x, f = vpad[:, :, k:k + L], filt[:, SHORT + k:SHORT + k + 1]
                        if k == 0:
                            V.tensor_scalar(longc[:, :, :], x, f, None, ALU.mult).then_inc(S["fir_steps"], 1)
                        else:
                            dve.wait_ge(S["fir_steps"], g * DVE_TAPS + k)
                            V.scalar_tensor_tensor(longc[:, :, :], x, f, longc[:, :, :], ALU.mult, ALU.add)\
                                .then_inc(S["fir_steps"], 1)

                V.memset(state[:, 0, :, :], 0.0).then_inc(S["s_zero"], 1)
                dve.wait_ge(S["s_zero"], g + 1)
                dve.wait_ge(S["blocks_out"], g * 3 + 3)
                for n in range(L // C):
                    share = range(n * DVE_TAPS * C // L, (n + 1) * DVE_TAPS * C // L)
                    dve.wait_ge(S["ws"], g * 8 + n + 1)
                    V.tensor_tensor(ui[:, :, :], uu[:, n:NB:L // C, :], ps[:, 0, 0:GS * D].rearrange("p (b d) -> p b d", b=GS),
                                    ALU.subtract).then_inc(S["ui"], 1)
                    long_taps(share[:1])
                    dve.wait_ge(S["sd"], g * 8 + n + 1)
                    V.scalar_tensor_tensor(state[:, (n + 1) % 2, :, :], state[:, n % 2, :, :], hv[:, 0:1],
                                           ps[:, 2, 0:GS * D].rearrange("p (b d) -> p b d", b=GS), ALU.mult, ALU.add)\
                        .then_inc(S["scan_s"], 1)
                    long_taps(share[1:])
                dve.wait_ge(S["fir_steps"], (g + 1) * DVE_TAPS)
                dve.wait_ge(S["fir_pe"], g + 1)
                V.tensor_tensor(longc[:, :, :], ps[:, 6:8, :].rearrange("p a (b t) -> p (a b) t", b=2), longc[:, :, :], ALU.add)\
                    .then_inc(S["fir_sum"], 1)
                dve.wait_ge(S["fir_sum"], g * 2 + 1)
                dve.wait_ge(S["pool_fir"], (g + 1) * (2 * POOL_TAPS - 1))
                V.tensor_tensor(longc[:, :, :], longc[:, :, :], longp[:, :, :], ALU.add).then_inc(S["fir_sum"], 1)
                dve.wait_ge(S["fir_sum"], g * 2 + 2)
                V.transpose(str4[:, 1, :, :].rearrange("p b d -> p (b d)"), longc[:, :, :].rearrange("p s t -> p (s t)"))\
                    .then_inc(S["streams"], 1)
                dve.wait_ge(S["streams"], g * 2 + 2)
                dve.wait_ge(S["o_out"], g * 8 + 8)
                mean_of(1, 3, 2)
                if not last:
                    turn_qk(g + 1)
                variance_of(1, 3, 2)
                dve.wait_ge(S["var_steps"], g * 9 + 9)
                dve.wait_ge(S["l2"], g + 1)
                dve.wait_ge(S["stat"], g * 3 + 3)
                V.transpose(statc[:, :], stat[:, :, :].rearrange("p b f -> p (b f)")).then_inc(S["statc"], 1)
                if not last:
                    unit_qk(g + 1)
                dve.wait_ge(S["lg"], g * 2 + 2)
                V.transpose(lt[:, :, :].rearrange("p b d -> p (b d)"), lg[:, :]).then_inc(S["lt"], 1)
                dve.wait_ge(S["lt"], g + 1)
                pmb = pm[:, :].unsqueeze(2).to_broadcast([P, NB, 4])
                steps = [0]

                def step(ins):
                    steps[0] += 1
                    ins.then_inc(S["sm_steps"], 1)
                    dve.wait_ge(S["sm_steps"], g * 10 + steps[0])

                step(V.tensor_scalar(pg[:, :, :], lt[:, :, 0:4], hv[:, 1:2], None, ALU.mult))
                step(V.tensor_reduce(pm[:, :], pg[:, :, :], AX.X, ALU.max))
                step(V.tensor_tensor(pg[:, :, :], pg[:, :, :], pmb, ALU.subtract))
                dve.wait_ge(S["exped"], g + 1)
                step(V.tensor_reduce(pm[:, :], pg[:, :, :], AX.X, ALU.add))
                step(V.reciprocal(pm[:, :], pm[:, :]))
                step(V.tensor_tensor(pg[:, :, :], pg[:, :, :], pmb, ALU.mult))
                step(V.tensor_tensor(pg[:, :, :], pg[:, :, :], hv[:, 4:8].unsqueeze(1).to_broadcast([P, NB, 4]), ALU.max))
                step(V.tensor_reduce(pm[:, :], pg[:, :, :], AX.X, ALU.add))
                step(V.reciprocal(pm[:, :], pm[:, :]))
                step(V.tensor_tensor(pg[:, :, :], pg[:, :, :], pmb, ALU.mult))
                for s in range(4):
                    V.tensor_tensor(cen[:, s * NB:(s + 1) * NB, :], str4[:, s, :, :],
                                    pg[:, :, s:s + 1].to_broadcast([P, NB, D]), ALU.mult).then_inc(S["mixed"], 1)
                dve.wait_ge(S["mixed"], g * 4 + 4)
                V.tensor_reduce(om[:, :, :].rearrange("p b d -> p (b d)"), cen[:, :, :].rearrange("p (s b) d -> p (b d) s", s=4),
                                AX.X, ALU.add).then_inc(S["om"], 1)
                if not last:
                    turn_beta(g + 1)
                dve.wait_ge(S["o_sq"], g + 1)
                V.tensor_reduce(orms[:, :], sqr[:, 0:NB, :], AX.X, ALU.add).then_inc(S["temp"], 1)
                dve.wait_ge(S["temp"], g * 2 + 1)
                V.tensor_scalar(orms[:, :], orms[:, :], 1.0 / D, 1e-5, ALU.mult, ALU.add).then_inc(S["temp"], 1)
                dve.wait_ge(S["temp"], g * 2 + 2)
                newton_rsqrt(nc, dve, orms[:, :], orr[:, :], ort[:, :], S["rms_steps"], g * NEWTON)
                dve.wait_ge(S["rms_steps"], g * NEWTON + NEWTON)
                V.tensor_tensor(om[:, :, :], om[:, :, :], orr[:, :].unsqueeze(2).to_broadcast([P, NB, D]), ALU.mult)\
                    .then_inc(S["o_norm"], 1)
                dve.wait_ge(S["o_norm"], g * 2 + 1)
                V.tensor_tensor(om[:, :, :], om[:, :, :], normw[:, :].unsqueeze(1).to_broadcast([P, NB, D]), ALU.mult)\
                    .then_inc(S["o_norm"], 1)
                dve.wait_ge(S["o_norm"], g * 2 + 2)
                V.transpose(oc[:, :], om[:, :, :].rearrange("p b d -> p (b d)")).then_inc(S["oc"], 1)
                if not last:
                    turn_v(g + 1)
                    below_diagonal(g + 1)
                dve.wait_ge(S["out"], g + 1)
                dve.wait_ge(S["x_in"], g * 16 + 16)
                V.tensor_tensor(res[:, :, :], ps[:, 0:2, :].rearrange("p a (b d) -> p (a b) d", b=4), xt[:, :, :], ALU.add)\
                    .then_inc(S["res"], 1)

            turn_qk(0)
            unit_qk(0)
            turn_beta(0)
            turn_v(0)
            below_diagonal(0)
            groups(dve, group)

        @block.tensor
        def _(pe):
            pe.wait_ge(S["prep"], 3)
            pe.wait_ge(S["loaded"], 16 * NLOAD)
            T = nc.tensor

            def blocks(bank, lhs, rhs, sem):
                T.matmul(ps[:, bank, 0:1], ident[:, :], ident[:, 0:1], start=True, stop=True)
                for b in range(NB):
                    for h in range(H):
                        r = slice(h * D, (h + 1) * D)
                        mm = T.matmul(ps[r, bank + b // 16, b % 16 * C:(b % 16 + 1) * C], lhs(r, b), rhs(r, b),
                                      start=True, stop=True)
                mm.then_inc(sem, 1)

            col = lambda t: (lambda r, b: t[r, b * C:(b + 1) * C])
            blk = lambda t: (lambda r, b: t[r, b, :])

            def product_kk(g):
                pe.wait_ge(S["unit_c"], g * 2 + 1)
                blocks(2, col(kc), col(kc), S["kk"])

            def project(g, i):
                for c in range(2):
                    for b in range(2):
                        for k in range(CONV - 1, -1, -1):
                            s = CONV - 1 - k
                            x = stateT[:, bass.ds(g * GS + 2 * c + b, 1), 0:L - s].rearrange("p a t -> p (a t)")
                            mm = T.matmul(ps[:, (4, 6, 4)[i] + c, b * L + s:(b + 1) * L], wtap[:, i, k, :], x,
                                          start=s == 0, stop=s == CONV - 1)
                    mm.then_inc(S["proj"], 1)

            def project_v_beta(g):
                pe.wait_ge(S["silu"], g * 6 + 2)
                project(g, 2)
                pe.wait_ge(S["silu"], g * 6 + 4)
                for c in range(2):
                    x = stateT[:, bass.ds(g * GS + 2 * c, 2), :].rearrange("p a t -> p (a t)")
                    T.matmul(ps[:, 6 + c, :], wbx[:, :, :].rearrange("p h d -> p (h d)"), x, start=True, stop=True)\
                        .then_inc(S["proj"], 1)

            def group(g, last):
                pe.wait_ge(S["res"], g + 1)
                pe.wait_ge(S["unit_c"], g * 2 + 2)
                blocks(0, col(kc), col(qc), S["pe_blocks"])
                pe.wait_ge(S["silu"], g * 6 + 6)
                pe.wait_ge(S["beta_ps_turned"], g + 1)
                for c in range(2):
                    for k in range(PE_TAPS):
                        o = LONG - PE_TAPS + k
                        mm = T.matmul(ps[:, 6 + c, :].rearrange("p (b t) -> p b t", b=2), diag[:, k, :],
                                      vpad[:, 2 * c:2 * c + 2, o:o + L], start=k == 0, stop=k == PE_TAPS - 1)
                mm.then_inc(S["fir_pe"], 1)
                pe.wait_ge(S["na"], g * 2 + 1)
                pe.wait_ge(S["tT"], g + 1)
                pe.wait_ge(S["vkb"], g * 2 + 2)
                blocks(4, blk(tT), lambda r, b: vkb[r, b, 0:D], S["pe_blocks"])
                blocks(2, lambda r, b: vkb[r, b, D:2 * D], blk(tT), S["pe_blocks"])
                pe.wait_ge(S["blocks_out"], g * 3 + 3)
                pe.wait_ge(S["s_zero"], g + 1)
                for n in range(L // C):
                    if n > 0:
                        pe.wait_ge(S["scan_s"], g * 8 + n)
                    T.matmul(ps[:, 0, 0:1], ident[:, :], ident[:, 0:1], start=True, stop=True)
                    for b in range(GS):
                        for h in range(H):
                            r = slice(h * D, (h + 1) * D)
                            mm = T.matmul(ps[r, 0, b * D:(b + 1) * D], wT[r, b * 8 + n, :], state[r, n % 2, b, :],
                                          start=True, stop=True)
                    mm.then_inc(S["ws"], 1)
                    pe.wait_ge(S["ui"], g * 8 + n + 1)
                    T.matmul(ps[:, 2, 0:1], ident[:, :], ident[:, 0:1], start=True, stop=True)
                    for b in range(GS):
                        for h in range(H):
                            r = slice(h * D, (h + 1) * D)
                            mm = T.matmul(ps[r, 2, b * D:(b + 1) * D], qk_t[r, 1, b * 8 + n, :], ui[r, b, :],
                                          start=True, stop=True)
                    mm.then_inc(S["sd"], 1)
                    if n > 0:
                        pe.wait_ge(S["o_out"], g * 8 + n)
                    T.matmul(ps[:, 1, 0:1], ident[:, :], ident[:, 0:1], start=True, stop=True)
                    for b in range(GS):
                        for h in range(H):
                            r = slice(h * D, (h + 1) * D)
                            T.matmul(ps[r, 1, b * D:(b + 1) * D], qc[r, (b * 8 + n) * C:(b * 8 + n + 1) * C],
                                     state[r, n % 2, b, :], start=True, stop=False)
                            mm = T.matmul(ps[r, 1, b * D:(b + 1) * D], atT[r, b * 8 + n, :], ui[r, b, :],
                                          start=False, stop=True)
                    mm.then_inc(S["od"], 1)
                if not last:
                    project(g + 1, 0)
                    pe.wait_ge(S["fir_sum"], g * 2 + 1)
                    project(g + 1, 1)
                pe.wait_ge(S["statc"], g + 1)
                pe.wait_ge(S["scan_s"], g * 8 + 8)
                for t in range(2):
                    x = stateT[:, bass.ds(g * GS + 2 * t, 2), :].rearrange("p a t -> p (a t)")
                    for c in range(2):
                        T.matmul(ps[:, 2 * t + c, :], w1a[:, c * P:(c + 1) * P], x, start=True, stop=False)
                        T.matmul(ps[:, 2 * t + c, :], w1b[:, c * P:(c + 1) * P], statc[:, t * CK:(t + 1) * CK],
                                 start=False, stop=True).then_inc(S["hmid"], 1)
                for t in range(2):
                    pe.wait_ge(S["gelu"], g * 4 + 2 * t + 2)
                    for c in range(2):
                        mm = T.matmul(ps[:, 2 * t, :], w2x[:, c, :], hm[:, c, t * CK:(t + 1) * CK], start=c == 0, stop=c == 1)
                    mm.then_inc(S["logit"], 1)
                if not last:
                    project_v_beta(g + 1)
                    pe.wait_ge(S["lg"], g * 2 + 2)
                    product_kk(g + 1)
                pe.wait_ge(S["oc"], g + 1)
                for t in range(GT // P):
                    mm = T.matmul(ps[:, t // 4, t % 4 * P:(t % 4 + 1) * P], oc[:, t * P:(t + 1) * P], wout[:, :],
                                  start=True, stop=True)
                mm.then_inc(S["out"], 1)

            project(0, 0)
            project(0, 1)
            project_v_beta(0)
            product_kk(0)
            groups(pe, group)


def local_transformer(nc, stateT, ident, wqkv_d, scales_d, wb_d, par_d, rot_d, mask_d):
    with ExitStack() as stack:
        def sb(name, shape, dt=F32):
            return stack.enter_context(nc.sbuf_tensor(name, shape, dt))

        stage = sb("stage", [P, 3 * INNER + 4 * DH])
        w_hi = sb("w_hi", [P, 3 * INNER], F32R)
        w_lo = sb("w_lo", [P, 3 * INNER], F32R)
        wo = sb("wo", [P, NPAIR, P])
        w1 = sb("w1", [P, 2, FCH, P])
        w2 = sb("w2", [P, FCH, P])
        stage_wo = stage[:, 0:INNER]
        stage_w1 = stage[:, INNER:INNER + 2 * FCH * P]
        stage_w2 = stage[:, INNER + 2 * FCH * P:INNER + 3 * FCH * P]
        par_all = sb("par_all", [P, DEPTH * NPAR])
        par = sb("par", [P, NPAR])
        rot_base = sb("rot_base", [P, 2, 4 * DH])
        rot = sb("rot", [P, 2, 4, DH])
        mask = sb("mask", [P, 2 * P + 2 * KW], BF16)
        ident_b = sb("ident_b", [P, P], BF16)
        mean_w = sb("mean_w", [P, P])
        xs_hi = sb("xs_hi", [P, 2, L], F32R)
        xs_lo = sb("xs_lo", [P, 2, L], F32R)
        rot_a = sb("rot_a", [P, 2, CK])
        rot_b = sb("rot_b", [P, 2, CK])
        sq = sb("sq", [P, CK])
        qk = sb("qk", [P, 8, CK])
        ss = sb("ss", [P, 8 * 8])
        rn = sb("rn", [P, 2, 8 * 8])
        rn_t = sb("rn_t", [P, 8 * 8])
        qT = sb("qT", [P, 2, NPAIR, L])
        kT = sb("kT", [P, 2, NPAIR, 2, L])
        v = sb("v", [P, 2, 2, INNER])
        pr0 = sb("pr0", [P, 4, 2, P])
        pr1 = sb("pr1", [P, 4, 2, L])
        negmax = sb("negmax", [P, 4, 4])
        psums = sb("psums", [P, 4, 4])
        prec = sb("prec", [P, 4, 4])
        pT0 = sb("pT0", [P, 2, 2, KW])
        pT1 = sb("pT1", [P, 2, 2, P])
        oT = sb("oT", [P, 2, NPAIR, L])
        xf = sb("xf", [P, L])
        xc = sb("xc", [P, L])
        xsq = sb("xsq", [P, L])
        xn = sb("xn", [P, L])
        var = sb("var", [P, 2])
        rstd = sb("rstd", [P, 2])
        rstd_t = sb("rstd_t", [P, 2])
        gate = sb("gate", [P, FCH, L])
        hid = sb("hid", [P, FCH, L])

        banks = [stack.enter_context(nc.psum_tensor(f"bank{i}", [P, CK], F32)) for i in range(8)]
        ps_proj, ps_turn, ps_s0, ps_s1, ps_p0, ps_p1, ps_o, ps_c = banks
        ps_s = [ps_s0, ps_s1]
        KEYS = [P, KW]
        MASK = [mask[:, 0:2 * P], mask[:, 2 * P:2 * P + 2 * KW]]

        S = {n: stack.enter_context(nc.semaphore("t_" + n)) for n in (
            "loaded_a", "loaded_b", "loaded_const", "prepared", "conv_hi", "conv_lo", "conv_act", "conv_dve",
            "rot_ready", "xs_hi_ready", "xs_lo_ready", "projected", "rotated", "squared", "summed",
            "ss_floored", "rn_steps", "added", "scaled", "turned", "turned_out", "v_projected", "v_out",
            "scored", "maxed", "exped", "reciped", "normed", "p_turned", "p_turned_out",
            "valued", "values_out", "wo_done", "x_added", "xf_ready", "mean_done", "centred",
            "centred_sq", "var_done", "var_eps", "rstd_steps", "rstd_spread", "x_scaled", "xn_ready",
            "c_mm", "gate_out", "gelu_done", "value_out", "hid_done", "y_done", "layer_out")}

        class Body:

            def __init__(self, layer, base, n, parity, edge=None, first=False, last=False):
                self.layer, self.m, self.n, self.q, self.edge = layer, base + n, n, parity, edge

                def has(k):
                    return not (first and edge + k < 0) and not (last and edge + k > NSEQ - 1)

                self.aq, self.at, self.b, self.bt, self.c2 = (has(k) for k in (2, 1, 0, -1, -2))
                self.switch = edge if edge is not None and not last else None

            def seq(self, k):
                return self.n + k if self.edge is None else (self.edge + k) % NSEQ

        def pipeline(eng, f):
            def layer(l, base, first):
                for e in (-2, -1, 0, 1):
                    f(Body(l, base, e, e % 2, e, first=first))
                with eng.Fori(0, (NSEQ - 4) // 2) as pair:
                    for q in range(2):
                        f(Body(l, base, pair * 2 + (2 + q), q))
            layer(0, 0, True)
            with eng.Fori(1, DEPTH) as l:
                layer(l, l * NSEQ, False)
            for e in (NSEQ - 2, NSEQ - 1, NSEQ, NSEQ + 1):
                f(Body(DEPTH - 1, NSEQ * (DEPTH - 1), e, e % 2, e, last=True))

        def chunk(j):
            return j % 2, j // 2 % 2, j // 4

        def turned_before(j):
            return 3 * (j // 2) + j % 2

        block = stack.enter_context(nc.Block())

        @block.sync
        def _(sp):
            sp.dma_start(par_all[:, :], par_d).then_inc(S["loaded_const"], 16)
            sp.dma_start(rot_base[:, :, :], rot_d.rearrange("(u p) n -> p u n", p=P)).then_inc(S["loaded_const"], 16)
            sp.dma_start(hid[:, :, :].rearrange("p c t -> p (c t)")[:, 0:2 * P + 2 * KW], mask_d).then_inc(S["loaded_const"], 16)
            for l in range(DEPTH):
                need(sp, S["conv_act"], l * 2)
                need(sp, S["conv_dve"], l * 2)
                sp.dma_start(stage[:, 0:3 * INNER], wqkv_d[l, :, :])\
                    .then_inc(S["loaded_a"], 16)
                sp.dma_start(stage[:, 3 * INNER:3 * INNER + 4 * DH],
                             scales_d[l:l + 1, :].to_broadcast([P, 4 * DH])).then_inc(S["loaded_a"], 16)
                sp.wait_ge(S["conv_hi"], l * 6 + 6)
                sp.wait_ge(S["conv_lo"], l * 6 + 6)
                sp.wait_ge(S["rot_ready"], l + 1)
                sp.dma_start(stage[:, 0:INNER + 3 * FCH * P], wb_d[l, :, :])\
                    .then_inc(S["loaded_b"], 16)

        @block.gpsimd
        def _(pool):
            nc.gpsimd.memset(kT[:, :, :, :, :], 0.0).then_inc(S["prepared"], 1)
            nc.gpsimd.memset(pr1[:, :, :, :], 0.0).then_inc(S["prepared"], 1)
            nc.gpsimd.memset(mean_w[:, :], 1.0 / P).then_inc(S["prepared"], 1)
            nc.gpsimd.memset(xf[:, :], 0.0).then_inc(S["prepared"], 1)
            nc.gpsimd.memset(xs_hi[:, :, :].bitcast(F32), 0.0).then_inc(S["prepared"], 1)
            nc.gpsimd.memset(xs_lo[:, :, :].bitcast(F32), 0.0).then_inc(S["prepared"], 1)
            nc.gpsimd.tensor_copy(ident_b[:, :], ident[:, :]).then_inc(S["prepared"], 1)
            pool.wait_ge(S["loaded_const"], 48)
            nc.gpsimd.tensor_copy(mask[:, :], hid[:, :, :].rearrange("p c t -> p (c t)")[:, 0:2 * P + 2 * KW])\
                .then_inc(S["prepared"], 1)

            def body(b):
                m, G, u1, u2 = b.m, b.m * 8, b.m + 1, b.m + 2
                for j in range(8):
                    if b.b if j >= 1 else b.bt:
                        i = (j - 1) % 4
                        need(pool, S["reciped"], G + j)
                        for half, pr in ((0, pr0[:, i, :, :]), (1, pr1[:, i, :, P - WIN:L])):
                            r = prec[:, i, 2 * half:2 * half + 2].unsqueeze(2).to_broadcast([P, 2, KEYS[half]])
                            nc.gpsimd.tensor_tensor(pr, pr, r, ALU.mult).then_inc(S["normed"], 1)
                    if b.at if j < 7 else b.aq:
                        u, c, uq = (u1, j + 1, 1 - b.q) if j < 7 else (u2, 0, b.q)
                        need(pool, S["rn_steps"], u * 2 * NEWTON + (c // 4 + 1) * NEWTON)
                        need(pool, S["added"], u * 8 + (c + 1))
                        x = qk[:, c, :].rearrange("p (h d) -> p h d", h=8)
                        nc.gpsimd.tensor_tensor(x, x, rn[:, uq, 8 * c:8 * c + 8].unsqueeze(2).to_broadcast([P, 8, DH]),
                                                ALU.mult).then_inc(S["scaled"], 1)
                    if b.aq:
                        need(pool, S["rotated"], u2 * 16 + (2 * j + 2))
                        need(pool, S["turned"], u1 * 8 + (j + 1) if b.at else 0)
                        nc.gpsimd.tensor_tensor(qk[:, j, :], rot_a[:, j % 2, :], rot_b[:, j % 2, :], ALU.add)\
                            .then_inc(S["added"], 1)

            pipeline(pool, body)

        @block.scalar
        def _(act):
            act.wait_ge(S["prepared"], 8)

            def convert(b, cols, first_user_done):
                need(act, S["loaded_a"], b.layer * 32 + 32)
                need(act, *first_user_done)
                for c in cols:
                    nc.scalar.activation(w_hi[:, c * CK:(c + 1) * CK], stage[:, c * CK:(c + 1) * CK], ACT.Copy)\
                        .then_inc(S["conv_hi"], 1)

            def body(b):
                m, G, u1, u2, uc = b.m, b.m * 8, b.m + 1, b.m + 2, b.m - 2
                if b.switch == -2:
                    convert(b, (0, 2, 1, 3), (S["projected"], u2 * 8))
                if b.switch == -1:
                    convert(b, (4, 5), (S["v_projected"], u1 * 4))
                if b.switch == 1:
                    need(act, S["loaded_b"], b.layer * 16 + 16)
                    need(act, S["wo_done"], m - 1)
                    nc.scalar.activation(wo[:, :, :].rearrange("p c n -> p (c n)"), stage_wo, ACT.Copy)\
                        .then_inc(S["conv_act"], 1)
                if b.aq:
                    if not (isinstance(b.layer, int) and b.layer == 0):
                        need(act, S["layer_out"], u2 - (NSEQ - 1))
                    need(act, S["v_projected"], (u2 - 1) * 4)
                    src = stateT[:, b.seq(2), :] if b.edge is not None else \
                        stateT[:, bass.ds(b.seq(2), 1), :].rearrange("p a t -> p (a t)")
                    nc.scalar.activation(xs_hi[0:DH, b.q, :], src[0:DH, :], ACT.Copy).then_inc(S["xs_hi_ready"], 1)
                    nc.scalar.activation(xs_hi[DH:P, b.q, 1:L], src[DH:P, 0:L - 1], ACT.Copy)\
                        .then_inc(S["xs_hi_ready"], 1)
                for j in range(8):
                    i = j % 4
                    if b.aq if j >= 1 else b.at:
                        u, c = (u2, j - 1) if j >= 1 else (u1, 7)
                        need(act, S["rotated"], u * 16 + (2 * c + 2))
                        need(act, S["summed"], u * 8 + c)
                        nc.scalar.activation(sq[:, :], ps_proj[:, :], ACT.Square).then_inc(S["squared"], 1)
                    for half in range(2):
                        if b.b:
                            need(act, S["maxed"], G + G + (2 * j + half + 1))
                            if half == 0:
                                need(act, S["p_turned"], G * 2 + (2 * j - 6))
                            for e in range(2):
                                out = pr0[:, i, e, :] if half == 0 else pr1[:, i, e, P - WIN:L]
                                k = 2 * half + e
                                ins = nc.scalar.activation(out, ps_s[half][:, e * KEYS[half]:(e + 1) * KEYS[half]], ACT.Exp,
                                                           bias=negmax[:, i, k:k + 1], accum_out=psums[:, i, k:k + 1])
                            ins.then_inc(S["exped"], 1)
                        if b.c2 and j == 0 and half == 0:
                            need(act, S["x_scaled"], uc + 1)
                            nc.scalar.activation(xn[:, :], xc[:, :], ACT.Identity, bias=par[:, NPAR - 1:NPAR],
                                                 scale=par[:, NPAR - 2:NPAR - 1]).then_inc(S["xn_ready"], 1)
                    if b.bt and j == 5:
                        need(act, S["x_added"], m)
                        need(act, S["centred"], m - 1)
                        src = stateT[:, b.seq(-1), :] if b.edge is not None else \
                            stateT[:, bass.ds(b.seq(-1), 1), :].rearrange("p a t -> p (a t)")
                        nc.scalar.activation(xf[0:DH, :], src[0:DH, :], ACT.Copy).then_inc(S["xf_ready"], 1)
                        nc.scalar.activation(xf[DH:P, 1:L], src[DH:P, 0:L - 1], ACT.Copy).then_inc(S["xf_ready"], 1)
                    if b.bt and j == 6:
                        need(act, S["centred"], m)
                        nc.scalar.activation(xsq[:, :], xc[:, :], ACT.Square).then_inc(S["centred_sq"], 1)
                    if b.b if j >= 2 else b.bt:
                        for n, (dst, src) in enumerate(((pT0[:, j % 2, :, :], ps_p0[:, 0:2 * KW]),
                                                        (pT1[:, j % 2, :, :], ps_p1[:, 0:2 * P]))):
                            need(act, S["p_turned"], G * 2 + (2 * (j - 2) + n + 1))
                            need(act, S["valued"], G + (j - 2 - 1))
                            nc.scalar.activation(dst.rearrange("p e t -> p (e t)"), src, ACT.Copy)\
                                .then_inc(S["p_turned_out"], 1)
                    if b.at:
                        kind, half, grp = chunk(j)
                        need(act, S["turned"], u1 * 8 + (j + 1))
                        need(act, S["scored"], m * 16)
                        src = ps_turn[:, :].rearrange("p (c t) -> p c t", c=4)
                        cols = slice(half * P, (half + 1) * P)
                        if kind == 0:
                            nc.scalar.activation(qT[:, 1 - b.q, 4 * grp:4 * grp + 4, cols], src, ACT.Copy)\
                                .then_inc(S["turned_out"], 1)
                        else:
                            for e in range(2):
                                r = slice(e * DH, (e + 1) * DH)
                                nc.scalar.activation(kT[r, 1 - b.q, 4 * grp:4 * grp + 4, e, cols], src[r, :, :], ACT.Copy)\
                                    .then_inc(S["turned_out"], 1)
                    if b.c2 and j == 2:
                        need(act, S["gate_out"], uc * 3 + 3)
                        nc.scalar.activation(gate[:, :, :], gate[:, :, :], ACT.Gelu).then_inc(S["gelu_done"], 1)
                    if b.switch == 1 and j == 5:
                        need(act, S["y_done"], m - 1)
                        nc.scalar.activation(w1[:, :, :, :].rearrange("p a c n -> p (a c n)"), stage_w1, ACT.Copy)\
                            .then_inc(S["conv_act"], 1)

            pipeline(act, body)

        @block.vector
        def _(dve):
            dve.wait_ge(S["loaded_const"], 48)
            dve.wait_ge(S["prepared"], 8)

            def convert(b, cols, first_conv):
                for n, c in enumerate(cols):
                    need(dve, S["conv_hi"], b.layer * 6 + (first_conv + n + 1))
                    x = slice(c * CK, (c + 1) * CK)
                    nc.vector.tensor_tensor(w_lo[:, x], stage[:, x], w_hi[:, x].bitcast(F32), ALU.subtract)\
                        .then_inc(S["conv_lo"], 1)

            def body(b):
                m, G, u1, u2, uc = b.m, b.m * 8, b.m + 1, b.m + 2, b.m - 2
                if b.switch == -2:
                    need(dve, S["loaded_a"], b.layer * 32 + 32)
                    need(dve, S["rotated"], u2 * 16)
                    nc.vector.tensor_tensor(
                        rot[:, :, :, :].rearrange("p u k d -> p u (k d)"), rot_base[:, :, :],
                        stage[:, 3 * INNER:3 * INNER + 4 * DH].unsqueeze(1).to_broadcast([P, 2, 4 * DH]),
                        ALU.mult).then_inc(S["rot_ready"], 1)
                    convert(b, (0, 2, 1, 3), 0)
                    need(dve, S["rot_ready"], b.layer + 1)
                if b.switch == -1:
                    convert(b, (4, 5), 4)

                def norm_step(j, step):
                    if not (b.at if j < 4 else b.aq) or j % 4 > 1 or (j % 4 == 0 and step < 0):
                        return
                    k = step if j % 4 == 0 else 7 + step
                    u, uq, cols = (u1, 1 - b.q, slice(32, 64)) if j < 4 else (u2, b.q, slice(0, 32))
                    if k == 0:
                        need(dve, S["summed"], u * 8 + (8 if j < 4 else 4))
                        nc.vector.tensor_scalar(ss[:, cols], ss[:, cols], 1e-24, None, ALU.max).then_inc(S["ss_floored"], 1)
                    else:
                        if k == 1:
                            need(dve, S["ss_floored"], u * 2 + (2 if j < 4 else 1))
                        newton_step(nc, dve, k - 1, ss[:, cols], rn[:, uq, cols], rn_t[:, cols], S["rn_steps"],
                                    u * 2 * NEWTON + (NEWTON if j < 4 else 0))

                def deviation_step(k):
                    if k == 0:
                        need(dve, S["var_done"], m)
                        nc.vector.tensor_scalar(var[:, :], ps_c[:, 0:2], 1e-5, None, ALU.add).then_inc(S["var_eps"], 1)
                    elif k <= NEWTON:
                        if k == 1:
                            need(dve, S["var_eps"], m)
                        newton_step(nc, dve, k - 1, var[:, :], rstd[:, :], rstd_t[:, :], S["rstd_steps"], (m - 1) * NEWTON)

                def between(j, place):
                    norm_step(j, place - 2)
                    if b.bt and j == 7:
                        deviation_step(2 * place)
                        deviation_step(2 * place + 1)

                for j in range(8):
                    i = j % 4
                    if b.switch == 1 and j == 6:
                        need(dve, S["conv_dve"], b.layer * 2 + 2)
                    for half in range(2):
                        if b.b:
                            need(dve, S["scored"], G * 2 + (2 * j + half + 1))
                            x = ps_s[half][:, 0:2 * KEYS[half]].rearrange("p (e k) -> p e k", e=2)
                            nc.vector.tensor_reduce(negmax[:, i, 2 * half:2 * half + 2], x, AX.X, ALU.max, negate=True)\
                                .then_inc(S["maxed"], 1)
                        between(j, half)
                    if b.c2:
                        if j == 0:
                            need(dve, S["rstd_spread"], uc + 1)
                            nc.vector.tensor_tensor(xc[:, :], xc[:, :], ps_c[:, 0:L], ALU.mult).then_inc(S["x_scaled"], 1)
                        if j in (1, 2):
                            need(dve, S["c_mm"], uc * 3 + j)
                            for c in ((0, 1) if j == 1 else (2,)):
                                nc.vector.tensor_scalar(gate[:, c, :], ps_c[:, (c % 2) * L:(c % 2 + 1) * L],
                                                        par[:, FCH + c:FCH + c + 1], None, ALU.add).then_inc(S["gate_out"], 1)
                        if j == 2:
                            nc.vector.tensor_scalar(hid[:, 0, :], ps_c[:, L:2 * L], par[:, 0:1], None, ALU.add)\
                                .then_inc(S["value_out"], 1)
                        if j == 4:
                            need(dve, S["y_done"], uc + 1)
                            dst = stateT[:, b.seq(-2), :] if b.edge is not None else \
                                stateT[:, bass.ds(b.seq(-2), 1), :].rearrange("p a t -> p (a t)")
                            nc.vector.scalar_tensor_tensor(dst, ps_c[:, 0:L], par[:, 2 * FCH:2 * FCH + 1], dst,
                                                           ALU.add, ALU.add).then_inc(S["layer_out"], 1)
                    if b.bt:
                        if j == 5:
                            need(dve, S["wo_done"], m)
                            dst = stateT[:, b.seq(-1), :] if b.edge is not None else \
                                stateT[:, bass.ds(b.seq(-1), 1), :].rearrange("p a t -> p (a t)")
                            nc.vector.tensor_tensor(dst, ps_c[:, 0:L], dst, ALU.add).then_inc(S["x_added"], 1)
                        if j == 6:
                            need(dve, S["mean_done"], m)
                            nc.vector.tensor_tensor(xc[:, :], xf[:, :], ps_c[:, 0:L], ALU.subtract).then_inc(S["centred"], 1)
                    if b.at and 3 <= j < 7:
                        half, c = (j - 3) // 2, (j - 3) % 2
                        need(dve, S["v_projected"], u1 * 4 + (j - 3 + 1))
                        need(dve, S["valued"], m * 8)
                        nc.vector.tensor_copy(v[:, 1 - b.q, half, c * CK:(c + 1) * CK], ps_turn[:, :])\
                            .then_inc(S["v_out"], 1)
                    if b.aq and j == 0:
                        need(dve, S["xs_hi_ready"], u2 * 2 + 2)
                        src = stateT[:, b.seq(2), :] if b.edge is not None else \
                            stateT[:, bass.ds(b.seq(2), 1), :].rearrange("p a t -> p (a t)")
                        nc.vector.tensor_tensor(xs_lo[0:DH, b.q, :], src[0:DH, :], xs_hi[0:DH, b.q, :].bitcast(F32),
                                                ALU.subtract).then_inc(S["xs_lo_ready"], 1)
                        nc.vector.tensor_tensor(xs_lo[DH:P, b.q, 1:L], src[DH:P, 0:L - 1],
                                                xs_hi[DH:P, b.q, 1:L].bitcast(F32), ALU.subtract)\
                            .then_inc(S["xs_lo_ready"], 1)
                    if b.aq if j >= 1 else b.at:
                        u, c = (u2, j - 1) if j >= 1 else (u1, 7)
                        need(dve, S["squared"], u * 8 + (c + 1))
                        nc.vector.tensor_reduce(ss[:, 8 * c:8 * c + 8], sq[:, :].rearrange("p (h d) -> p h d", h=8),
                                                AX.X, ALU.add).then_inc(S["summed"], 1)
                    between(j, 2)
                    if b.c2 and j == 3:
                        need(dve, S["gelu_done"], uc + 1)
                        need(dve, S["value_out"], uc + 1)
                        nc.vector.tensor_tensor(hid[:, 0, :], hid[:, 0, :], gate[:, 0, :], ALU.mult).then_inc(S["hid_done"], 1)
                        need(dve, S["c_mm"], uc * 3 + 3)
                        for c in (1, 2):
                            nc.vector.scalar_tensor_tensor(hid[:, c, :], ps_c[:, (c - 1) * L:c * L], par[:, c:c + 1],
                                                           gate[:, c, :], ALU.add, ALU.mult).then_inc(S["hid_done"], 1)
                    if b.b:
                        need(dve, S["exped"], G * 2 + (2 * j + 2))
                        need(dve, S["normed"], G * 2 + (2 * j - 6))
                        nc.vector.reciprocal(prec[:, i, :], psums[:, i, :]).then_inc(S["reciped"], 1)
                    between(j, 3)
                    if b.b if j >= 3 else b.bt:
                        g = j - 3
                        uq = b.q if j >= 3 else 1 - b.q
                        need(dve, S["valued"], G + (g + 1))
                        need(dve, S["wo_done"], m - 1)
                        nc.vector.tensor_copy(oT[:, uq, g % 8, :], ps_o[:, 0:L]).then_inc(S["values_out"], 1)
                    between(j, 4)
                    if b.switch == 1 and j == 5:
                        need(dve, S["loaded_b"], b.layer * 16 + 16)
                        need(dve, S["layer_out"], m - 1)
                        need(dve, S["xn_ready"], m - 1)
                        nc.vector.tensor_copy(w2[:, :, :].rearrange("p c n -> p (c n)"), stage_w2).then_inc(S["conv_dve"], 1)
                        src = par_all[:, 0:NPAR] if isinstance(b.layer, int) else par_all[:, bass.ds(b.layer * NPAR, NPAR)]
                        nc.vector.tensor_copy(par[:, :], src).then_inc(S["conv_dve"], 1)
                    if b.aq:
                        kind, half, grp = chunk(j)
                        need(dve, S["projected"], u2 * 8 + (j + 1))
                        need(dve, S["added"], u2 * 8 + (j - 1))
                        x = ps_proj[:, :].rearrange("p (h a d) -> p h a d", h=8, a=2)
                        cos = rot[:, half, 2 * kind, :].unsqueeze(1).to_broadcast([P, 8, DH])
                        sin = rot[:, half, 2 * kind + 1, :].rearrange("p (a d) -> p a d", a=2).unsqueeze(1)\
                            .to_broadcast([P, 8, 2, DH // 2])
                        nc.vector.tensor_tensor(rot_a[:, j % 2, :].rearrange("p (h d) -> p h d", h=8),
                                                ps_proj[:, :].rearrange("p (h d) -> p h d", h=8), cos, ALU.mult)\
                            .then_inc(S["rotated"], 1)
                    between(j, 5)
                    if b.aq:
                        nc.vector.tensor_tensor(rot_b[:, j % 2, :].rearrange("p (h a d) -> p h a d", h=8, a=2),
                                                x[:, :, ::-1, :], sin, ALU.mult).then_inc(S["rotated"], 1)
                    between(j, 6)

            pipeline(dve, body)

        @block.tensor
        def _(pe):
            pe.wait_ge(S["loaded_const"], 48)
            pe.wait_ge(S["prepared"], 8)

            def project(out, q, half, cols):
                for n, (x, w) in enumerate(((xs_hi, w_hi), (xs_lo, w_hi), (xs_hi, w_lo))):
                    mm = nc.tensor.matmul(out[:, :], x[:, q, half * P:(half + 1) * P], w[:, cols:cols + CK],
                                          start=n == 0, stop=n == 2)
                return mm

            def body(b):
                m, G, u1, u2, uc = b.m, b.m * 8, b.m + 1, b.m + 2, b.m - 2
                for j in range(8):
                    if b.b:
                        if j in (0, 4):
                            need(pe, S["turned_out"], m * 12 + (6 * (j // 4) + 6))
                        for half in range(2):
                            need(pe, S["exped"], G * 2 + (2 * j - 2 + half + 1))
                            kn = KEYS[half]
                            nc.tensor.matmul(ps_s[half][:, 0:2 * kn], ident_b[:, :], MASK[half], start=True, stop=False)
                            nc.tensor.matmul(ps_s[half][:, 0:2 * kn].rearrange("p (e k) -> p e k", e=2),
                                             qT[:, b.q, j, half * P:(half + 1) * P],
                                             kT[:, b.q, j, :, (half + 1) * P - kn:(half + 1) * P],
                                             start=False, stop=True).then_inc(S["scored"], 1)
                    if b.at and 3 <= j < 7:
                        half, c = (j - 3) // 2, (j - 3) % 2
                        need(pe, S["turned_out"], u1 * 12 + turned_before(j))
                        if b.switch == -1 and j in (3, 4):
                            need(pe, S["conv_lo"], b.layer * 6 + (4 + c + 1))
                        project(ps_turn, 1 - b.q, half, 2 * INNER + c * CK).then_inc(S["v_projected"], 1)
                    if b.c2 and j == 0:
                        need(pe, S["rstd_steps"], uc * NEWTON + NEWTON)
                        for c in range(2):
                            mm = nc.tensor.matmul(ps_c[:, c * P:(c + 1) * P], rstd[:, c:c + 1].to_broadcast([P, P]), ident[:, :],
                                                  start=True, stop=True)
                        mm.then_inc(S["rstd_spread"], 1)
                    if b.b if j >= 2 else b.bt:
                        g, i = j - 2, (j - 2) % 4
                        need(pe, S["normed"], G * 2 + (2 * g + 2))
                        need(pe, S["p_turned_out"], G * 2 + (2 * g - 1))
                        for e in range(2):
                            nc.tensor.transpose(ps_p0[:, e * KW:e * KW + P], pr0[:, i, e, :], ident[:, :])
                            mm = nc.tensor.transpose(ps_p0[:, e * KW + P:(e + 1) * KW], pr1[0:WIN, i, e, 0:P],
                                                     ident[0:WIN, 0:WIN])
                        mm.then_inc(S["p_turned"], 1)
                        need(pe, S["p_turned_out"], G * 2 + 2 * g)
                        for e in range(2):
                            mm = nc.tensor.transpose(ps_p1[:, e * P:(e + 1) * P], pr1[:, i, e, P:L], ident[:, :])
                        mm.then_inc(S["p_turned"], 1)
                    if b.b if j >= 3 else b.bt:
                        g = j - 3
                        uq = b.q if j >= 3 else 1 - b.q
                        need(pe, S["p_turned_out"], G * 2 + (2 * g + 2))
                        need(pe, S["v_out"], (m if j >= 3 else m - 1) * 4 + 4)
                        need(pe, S["values_out"], G + g)
                        for e in range(2):
                            r = slice(e * DH, (e + 1) * DH)
                            c = (2 * (g % 8) + e) * DH
                            nc.tensor.matmul(ps_o[r, 0:KW], v[:, uq, 0, c:c + DH], pT0[:, (j - 1) % 2, e, :],
                                             start=True, stop=False, skip_group_check=True)
                            mm = nc.tensor.matmul(ps_o[r, P:L], v[:, uq, 1, c:c + DH], pT1[:, (j - 1) % 2, e, :],
                                                  start=False, stop=True, skip_group_check=True)
                        mm.then_inc(S["valued"], 1)
                    if b.at:
                        need(pe, S["scaled"], u1 * 8 + (j + 1))
                        if 3 <= j < 7:
                            need(pe, S["v_out"], u1 * 4 + (j - 3 + 1))
                        else:
                            need(pe, S["turned_out"], u1 * 12 + turned_before(j))
                        for c in range(4):
                            mm = nc.tensor.transpose(ps_turn[:, c * P:(c + 1) * P], qk[:, j, c * P:(c + 1) * P], ident[:, :])
                        mm.then_inc(S["turned"], 1)
                    if b.aq:
                        kind, half, grp = chunk(j)
                        need(pe, S["rotated"], u2 * 16 + 2 * j)
                        need(pe, S["squared"], u2 * 8 + j)
                        if j == 0:
                            need(pe, S["xs_lo_ready"], u2 * 2 + 2)
                        if b.switch == -2 and j in (0, 1, 4, 5):
                            need(pe, S["conv_lo"], b.layer * 6 + (j + 1 if j < 2 else j - 1))
                        project(ps_proj, b.q, half, kind * INNER + grp * CK).then_inc(S["projected"], 1)
                    if b.switch == 1 and j == 6:
                        need(pe, S["conv_act"], b.layer * 2 + 2)
                        need(pe, S["conv_dve"], b.layer * 2 + 2)
                    if b.c2:
                        if j == 0:
                            need(pe, S["xn_ready"], uc + 1)
                            for c in range(2):
                                mm = nc.tensor.matmul(ps_c[:, c * L:(c + 1) * L], w1[:, 1, c, :], xn[:, :], start=True, stop=True)
                            mm.then_inc(S["c_mm"], 1)
                        if j == 1:
                            need(pe, S["gate_out"], uc * 3 + 2)
                            nc.tensor.matmul(ps_c[:, 0:L], w1[:, 1, 2, :], xn[:, :], start=True, stop=True)
                            nc.tensor.matmul(ps_c[:, L:2 * L], w1[:, 0, 0, :], xn[:, :], start=True, stop=True)\
                                .then_inc(S["c_mm"], 1)
                        if j == 2:
                            need(pe, S["gate_out"], uc * 3 + 3)
                            need(pe, S["value_out"], uc + 1)
                            for c in (1, 2):
                                mm = nc.tensor.matmul(ps_c[:, (c - 1) * L:c * L], w1[:, 0, c, :], xn[:, :], start=True, stop=True)
                            mm.then_inc(S["c_mm"], 1)
                        if j == 3:
                            need(pe, S["hid_done"], uc * 3 + 3)
                            for c in range(FCH):
                                mm = nc.tensor.matmul(ps_c[:, 0:L], w2[:, c, :], hid[:, c, :], start=c == 0, stop=c == FCH - 1)
                            mm.then_inc(S["y_done"], 1)
                    if b.bt:
                        if j == 4:
                            need(pe, S["values_out"], m * 8)
                            need(pe, S["layer_out"], m - 1)
                            if b.switch == 1:
                                need(pe, S["conv_act"], b.layer * 2 + 1)
                            for c in range(NPAIR):
                                mm = nc.tensor.matmul(ps_c[:, 0:L], wo[:, c, :], oT[:, 1 - b.q, c, :],
                                                      start=c == 0, stop=c == NPAIR - 1)
                            mm.then_inc(S["wo_done"], 1)
                        if j == 5:
                            need(pe, S["xf_ready"], m * 2)
                            nc.tensor.matmul(ps_c[:, 0:L], mean_w[:, :], xf[:, :], start=True, stop=True)\
                                .then_inc(S["mean_done"], 1)
                        if j == 6:
                            need(pe, S["centred_sq"], m)
                            for c in range(2):
                                mm = nc.tensor.matmul(ps_c[:, c:c + 1], xsq[:, c * P:(c + 1) * P], mean_w[:, 0:1],
                                                      start=True, stop=True)
                            mm.then_inc(S["var_done"], 1)

            pipeline(pe, body)


def write_output(nc, stateT, ident, base_d, out_d):
    with ExitStack() as stack:
        base = stack.enter_context(nc.sbuf_tensor("o_base", [P, NT, P], F32))
        ps = [stack.enter_context(nc.psum_tensor(f"o_ps{i}", [P, 4, P], F32)) for i in range(2)]
        s_in, s_turn, s_sum, s_out = (stack.enter_context(nc.semaphore("o_" + n)) for n in ("in", "turn", "sum", "out"))
        block = stack.enter_context(nc.Block())
        out_v = out_d.rearrange("b (u p) d -> p (b u) d", p=P)

        @block.sync
        def _(sp):
            sp.dma_start(base[:, :, :], base_d).then_inc(s_in, 16)
            for c in range(4):
                sp.wait_ge(s_sum, 2 * (c + 1))
                sp.dma_start(out_v[:, 8 * c:8 * c + 8, :], base[:, 8 * c:8 * c + 8, :]).then_inc(s_out, 16)
            sp.wait_ge(s_out, 64)

        @block.tensor
        def _(pe):
            for g in range(NT // 4):
                if g >= 2:
                    pe.wait_ge(s_sum, g - 1)
                for a in range(4):
                    t = 4 * g + a
                    mm = nc.tensor.transpose(ps[g % 2][:, a, :], stateT[:, t // 2, t % 2 * P:(t % 2 + 1) * P], ident[:, :])
                mm.then_inc(s_turn, 1)

        @block.vector
        def _(dve):
            dve.wait_ge(s_in, 16)
            for g in range(NT // 4):
                dve.wait_ge(s_turn, g + 1)
                nc.vector.tensor_tensor(base[:, 4 * g:4 * g + 4, :], ps[g % 2][:, :, :], base[:, 4 * g:4 * g + 4, :], ALU.add)\
                    .then_inc(s_sum, 1)


def program(nc, a, out_d):
    stateT = nc.alloc_sbuf_tensor("stateT", [P, NSEQ, L], F32)
    ident = nc.alloc_sbuf_tensor("ident", [P, P], F32)
    base_d = nc.dram_tensor("base_scratch", [P, NT, P], F32, kind="Internal").ap()
    with ExitStack() as stack:
        s_id = stack.enter_context(nc.semaphore("s_id"))
        with nc.Block() as block:
            @block.gpsimd
            def _(pool):
                nc.gpsimd.memset(ident[:, :], 0.0).then_inc(s_id, 1)
                pool.wait_ge(s_id, 1)
                nc.gpsimd.affine_select(out=ident[:, :], in_=ident[:, :], compare_op=ALU.not_equal, fill=1.0,
                                        base=0, pattern=[[-1, P]], channel_multiplier=1).then_inc(s_id, 1)
                pool.wait_ge(s_id, 2)
    normalise_input(nc, a["x"], stateT, ident)
    delta_mixer(nc, a["x"], stateT, ident, a, base_d)
    local_transformer(nc, stateT, ident, a["wqkv"], a["scales"], a["wb_all"], a["par"], a["rot"], a["mask"])
    write_output(nc, stateT, ident, base_d, out_d)


def shape_constants():
    f = np.float32
    half = np.arange(0, DH, 2, dtype=f)
    inv_freq = (f(1.0) / np.power(f(10000.0), half / f(DH))).astype(f)
    t = np.arange(L, dtype=f)
    freqs = t[:, None] * inv_freq[None, :]
    base = (half + f(0.4 * DH)) / f(1.4 * DH)
    power = (t - f(L // 2)) / f(WIN // 2)
    scale = np.power(base[None, :], power[:, None]).astype(f)
    cos, sin = np.cos(freqs).astype(f), np.sin(freqs).astype(f)
    both = lambda m: np.concatenate([m, m], -1)
    turned = lambda m: np.concatenate([-m, m], -1)
    inv = f(1.0) / scale
    rot = np.stack([both(cos * scale) * f(8), turned(sin * scale) * f(8), both(cos * inv), turned(sin * inv)], 1)
    i = np.arange(P)[:, None]
    masks = []
    for keys, first in ((P, 0), (KW, -WIN)):
        gap = i - (np.arange(keys)[None, :] + first)
        masks += [np.where((gap >= 0) & (gap <= WIN), 0.0, NEG)] * 2
    mask = np.concatenate(masks, 1).astype(f)
    r, c = np.arange(P)[:, None] % C, np.arange(C)[None, :]
    return {"rot": np.ascontiguousarray(rot.reshape(L, 4 * DH).astype(f)), "mask": mask,
            "below": np.where(c < r, -1.0, 0.0).astype(f), "upto": np.where(r <= c, 1.0, 0.0).astype(f)}


def lay_out(i):
    g = {k: np.asarray(v) for k, v in i.items()}
    A, B = "L0_attn_", "L0_ffn_"
    z = lambda *s: np.zeros(s, np.float32)
    a = {"x": g[A + "hidden_states"]}
    a["wqkv"] = g[B + "Wqkv"]
    swap = lambda m: np.concatenate([m[:, DH // 2:], m[:, :DH // 2]], 1)
    qs, ks = g[B + "q_scale"], g[B + "k_scale"]
    a["scales"] = np.stack([qs, swap(qs), ks, swap(ks)], 1).reshape(DEPTH, 4 * DH)
    w1 = z(DEPTH, P, 2, FCH * P)
    w1[:, :, :, :FFN] = g[B + "W1"].reshape(DEPTH, P, 2, FFN)
    w2 = z(DEPTH, FCH * P, P)
    w2[:, :FFN] = g[B + "W2"]
    chunks = lambda m, n: m.reshape(DEPTH, n, P, P).transpose(0, 2, 1, 3).reshape(DEPTH, P, n * P)
    a["wb_all"] = np.concatenate([chunks(g[B + "Wo"], NPAIR), w1.reshape(DEPTH, P, 2 * FCH * P), chunks(w2, FCH)], 2)
    b1 = z(DEPTH, 2, FCH * P)
    b1[:, :, :FFN] = g[B + "b1"].reshape(DEPTH, 2, FFN)
    par = np.concatenate([b1.reshape(DEPTH, 2 * FCH, P)] + [g[B + n][:, None] for n in ("b2", "ln_g", "ln_b")], 1)
    a["par"] = par.transpose(2, 0, 1).reshape(P, DEPTH * NPAR)
    a["wproj"] = np.stack([g[A + n] for n in ("Wq", "Wk", "Wv")], 1)
    a["taps"] = np.stack([g[A + n].T for n in ("conv_q", "conv_k", "conv_v")]).reshape(1, 3 * CONV * P)
    a["wb"] = g[A + "Wb"]
    a["filt"] = np.concatenate([g[A + "fir_short_w"].reshape(P, SHORT), g[A + "fir_long_w"].reshape(P, LONG)], 1)
    a["heads"] = np.repeat(np.concatenate([g[A + "forget_param"][:, None], g[A + "log_temp"][:, None],
                                           g[A + "floor_param"]], 1), D, 0)
    ws = z(H, D, 2 * P)
    ws[:, :16] = g[A + "W1"][P:].reshape(4, H, 4, 2 * P).transpose(1, 0, 2, 3).reshape(H, 16, 2 * P)
    a["w1"] = np.concatenate([g[A + "W1"][:P], ws.reshape(P, 2 * P)], 0)
    a["b1"] = g[A + "b1"].reshape(2, P).T
    w2x = z(2 * P, H, D)
    w2x[:, :, :4] = g[A + "W2"].reshape(2 * P, H, 4)
    a["w2x"] = w2x.reshape(2, P, P).transpose(1, 0, 2)
    b2x = z(H, D)
    b2x[:, :4] = g[A + "b2"].reshape(H, 4)
    a["b2x"] = b2x.reshape(P, 1)
    a["normw"] = g[A + "norm_w"].reshape(1, D)
    a["wout"] = g[A + "Wo"]
    a.update(shape_constants())
    return {k: np.ascontiguousarray(v) for k, v in a.items()}


def kernel(**inputs):
    import concourse.bacc as bacc
    from concourse.bass_utils import run_bass_kernel_spmd

    nc = bacc.Bacc("TRN2", target_bir_lowering=False, num_devices=1)
    arrays = lay_out(inputs)
    args = {k: nc.dram_tensor("in_" + k, v.shape, mybir.dt.from_np(v.dtype), kind="ExternalInput").ap()
            for k, v in arrays.items()}
    out = nc.dram_tensor("out", (NSEQ, L, P), F32, kind="ExternalOutput").ap()
    program(nc, args, out)
    r = run_bass_kernel_spmd(nc, [{"in_" + k: v for k, v in arrays.items()}], core_ids=[0])
    return r.results[0]["out"]
```
